# Optimizing a Trainium2 kernel written in Bass

```python
import numpy as np
import jax
import jax.numpy as jnp

def _softmax(x, axis=-1):
    return jax.nn.softmax(x, axis=axis)

def _gelu(x):
    return jax.nn.gelu(x, approximate=True)

def _silu(x):
    return jax.nn.silu(x)

def _sigmoid(x):
    return jax.nn.sigmoid(x)

def _layernorm(x, axis=-1, eps=1e-05):
    m = jnp.mean(x, axis=axis, keepdims=True)
    v = jnp.var(x, axis=axis, keepdims=True)
    return (x - m) / jnp.sqrt(v + eps)

def _scatter_add(tgt, idx, src, axis=0):
    return tgt.at[idx].add(src)

def _segment_sum(src, seg, n):
    return jax.ops.segment_sum(src, seg, n)
kernel_name = 'mk_prb_d1_jaxref_r4_551a56'

def setup_inputs(seed: int=0):
    np.random.seed(seed)
    _w = jnp.asarray

    def _L0_attn_setup():
        import jax, jax.numpy as jnp
        import numpy as np
        EPS = 1e-06
        CAP = 15.0
        NH = 8

        def soft_cap(x, cap=CAP):
            return cap * jnp.tanh(x / cap)

        def _mlstm_scan(q, k, v, i_pre, f_pre):
            B, S, nh, DQ = q.shape
            DV = v.shape[-1]
            scale = DQ ** (-0.5)

            def step(carry, xs):
                C, n, m = carry
                q_t, k_t, v_t, i_t, f_t = xs
                f_log = jax.nn.log_sigmoid(f_t)
                m_new = jnp.maximum(f_log + m, i_t)
                F = jnp.exp(f_log + m - m_new)
                I = jnp.exp(i_t - m_new)
                C_new = F[..., None, None] * C + (I[..., None] * k_t)[..., :, None] * v_t[..., None, :]
                n_new = F[..., None] * n + I[..., None] * k_t
                qs = q_t * scale
                h_num = jnp.einsum('bhd,bhdv->bhv', qs, C_new)
                qn = jnp.einsum('bhd,bhd->bh', qs, n_new)
                denom = jnp.maximum(jnp.abs(qn), jnp.exp(-m_new)) + EPS
                h = h_num / denom[..., None]
                return ((C_new, n_new, m_new), h)
            C0 = jnp.zeros((B, nh, DQ, DV), q.dtype)
            n0 = jnp.zeros((B, nh, DQ), q.dtype)
            m0 = jnp.zeros((B, nh), q.dtype)
            to_s = lambda a: jnp.moveaxis(a, 1, 0)
            (Cf, nf, mf), hs = jax.lax.scan(step, (C0, n0, m0), (to_s(q), to_s(k), to_s(v), to_s(i_pre), to_s(f_pre)))
            return (jnp.moveaxis(hs, 0, 1), (Cf, nf, mf))

        def _multihead_norm(h, gamma):
            h32 = h.astype(jnp.float32)
            mu = jnp.mean(h32, axis=-1, keepdims=True)
            var = jnp.mean((h32 - mu) ** 2, axis=-1, keepdims=True)
            hn = (h32 - mu) * jax.lax.rsqrt(var + EPS)
            return (hn * gamma).astype(h.dtype)

        def _reference_tuple_inner(x, Wq, Wk, Wv, Wog, Wig, big, Wfg, bfg, gamma, Wout):
            B, S, D = x.shape
            q = x @ Wq.T
            k = x @ Wk.T
            v = x @ Wv.T
            o_preact = x @ Wog.T
            i_pre = soft_cap(x @ Wig.T + big)
            f_pre = soft_cap(x @ Wfg.T + bfg)
            q = q.reshape(B, S, NH, -1)
            k = k.reshape(B, S, NH, -1)
            v = v.reshape(B, S, NH, -1)
            h, state = _mlstm_scan(q, k, v, i_pre, f_pre)
            h_norm = _multihead_norm(h, gamma).reshape(B, S, -1)
            h_out = jax.nn.sigmoid(o_preact) * h_norm
            y = h_out @ Wout.T
            return (y, *state)
        key = jax.random.key(seed)
        ks = jax.random.split(key, 12)
        B, S, D = (2, 512, 512)
        QK, V = (D // 2, D)
        DHV = V // NH
        s = lambda fan_in: 1.0 / np.sqrt(fan_in)
        return {'x': jax.random.normal(ks[0], (B, S, D), jnp.float32), 'Wq': jax.random.normal(ks[1], (QK, D), jnp.float32) * s(D), 'Wk': jax.random.normal(ks[2], (QK, D), jnp.float32) * s(D), 'Wv': jax.random.normal(ks[3], (V, D), jnp.float32) * s(D), 'Wog': jax.random.normal(ks[4], (V, D), jnp.float32) * s(D), 'Wig': jax.random.normal(ks[5], (NH, D), jnp.float32) * s(D), 'big': jax.random.normal(ks[6], (NH,), jnp.float32) * 0.1, 'Wfg': jax.random.normal(ks[7], (NH, D), jnp.float32) * s(D), 'bfg': jax.random.normal(ks[8], (NH,), jnp.float32) * 0.1 + 3.0, 'gamma': jnp.ones((NH, DHV), jnp.float32), 'Wout': jax.random.normal(ks[9], (D, V), jnp.float32) * s(V)}
    _L0_attn_in = _L0_attn_setup()

    def _L0_ffn_setup():
        import jax, jax.numpy as jnp
        import numpy as np
        DIM_IN = 512
        DIM_HIDDEN = 2048
        key = jax.random.key(seed)
        k_x, k_g, k_u, k_d = jax.random.split(key, 4)
        s_in = 1.0 / np.sqrt(DIM_IN)
        s_hid = 1.0 / np.sqrt(DIM_HIDDEN)
        x = jax.random.normal(k_x, (4, 512, DIM_IN), dtype=jnp.float32)
        w_gate = jax.random.uniform(k_g, (DIM_HIDDEN, DIM_IN), jnp.float32, -s_in, s_in)
        w_up = jax.random.uniform(k_u, (DIM_HIDDEN, DIM_IN), jnp.float32, -s_in, s_in)
        w_down = jax.random.uniform(k_d, (DIM_IN, DIM_HIDDEN), jnp.float32, -s_hid, s_hid)
        return {'x': x, 'w_gate': w_gate, 'w_up': w_up, 'w_down': w_down}
    _L0_ffn_in = _L0_ffn_setup()
    _d = {'L0_attn_x': _L0_attn_in['x'], 'L0_attn_Wq': _L0_attn_in['Wq'], 'L0_attn_Wk': _L0_attn_in['Wk'], 'L0_attn_Wv': _L0_attn_in['Wv'], 'L0_attn_Wog': _L0_attn_in['Wog'], 'L0_attn_Wig': _L0_attn_in['Wig'], 'L0_attn_big': _L0_attn_in['big'], 'L0_attn_Wfg': _L0_attn_in['Wfg'], 'L0_attn_bfg': _L0_attn_in['bfg'], 'L0_attn_gamma': _L0_attn_in['gamma'], 'L0_attn_Wout': _L0_attn_in['Wout'], 'L0_ffn_w_gate': _L0_ffn_in['w_gate'], 'L0_ffn_w_up': _L0_ffn_in['w_up'], 'L0_ffn_w_down': _L0_ffn_in['w_down']}
    _x0 = _d['L0_attn_x']
    _d['L0_attn_x'] = jax.random.normal(jax.random.fold_in(jax.random.key(seed), 1), (8, 1024, 512), dtype=_x0.dtype)
    del _x0
    return _d

def reference(L0_attn_x, L0_attn_Wq, L0_attn_Wk, L0_attn_Wv, L0_attn_Wog, L0_attn_Wig, L0_attn_big, L0_attn_Wfg, L0_attn_bfg, L0_attn_gamma, L0_attn_Wout, L0_ffn_w_gate, L0_ffn_w_up, L0_ffn_w_down):

    def _L0_attn_ref(x, Wq, Wk, Wv, Wog, Wig, big, Wfg, bfg, gamma, Wout):
        import jax, jax.numpy as jnp
        import numpy as np
        EPS = 1e-06
        CAP = 15.0
        NH = 8

        def soft_cap(x, cap=CAP):
            return cap * jnp.tanh(x / cap)

        def _mlstm_scan(q, k, v, i_pre, f_pre):
            B, S, nh, DQ = q.shape
            DV = v.shape[-1]
            scale = DQ ** (-0.5)

            def step(carry, xs):
                C, n, m = carry
                q_t, k_t, v_t, i_t, f_t = xs
                f_log = jax.nn.log_sigmoid(f_t)
                m_new = jnp.maximum(f_log + m, i_t)
                F = jnp.exp(f_log + m - m_new)
                I = jnp.exp(i_t - m_new)
                C_new = F[..., None, None] * C + (I[..., None] * k_t)[..., :, None] * v_t[..., None, :]
                n_new = F[..., None] * n + I[..., None] * k_t
                qs = q_t * scale
                h_num = jnp.einsum('bhd,bhdv->bhv', qs, C_new)
                qn = jnp.einsum('bhd,bhd->bh', qs, n_new)
                denom = jnp.maximum(jnp.abs(qn), jnp.exp(-m_new)) + EPS
                h = h_num / denom[..., None]
                return ((C_new, n_new, m_new), h)
            C0 = jnp.zeros((B, nh, DQ, DV), q.dtype)
            n0 = jnp.zeros((B, nh, DQ), q.dtype)
            m0 = jnp.zeros((B, nh), q.dtype)
            to_s = lambda a: jnp.moveaxis(a, 1, 0)
            (Cf, nf, mf), hs = jax.lax.scan(step, (C0, n0, m0), (to_s(q), to_s(k), to_s(v), to_s(i_pre), to_s(f_pre)))
            return (jnp.moveaxis(hs, 0, 1), (Cf, nf, mf))

        def _multihead_norm(h, gamma):
            h32 = h.astype(jnp.float32)
            mu = jnp.mean(h32, axis=-1, keepdims=True)
            var = jnp.mean((h32 - mu) ** 2, axis=-1, keepdims=True)
            hn = (h32 - mu) * jax.lax.rsqrt(var + EPS)
            return (hn * gamma).astype(h.dtype)

        def _reference_tuple_inner(x, Wq, Wk, Wv, Wog, Wig, big, Wfg, bfg, gamma, Wout):
            B, S, D = x.shape
            q = x @ Wq.T
            k = x @ Wk.T
            v = x @ Wv.T
            o_preact = x @ Wog.T
            i_pre = soft_cap(x @ Wig.T + big)
            f_pre = soft_cap(x @ Wfg.T + bfg)
            q = q.reshape(B, S, NH, -1)
            k = k.reshape(B, S, NH, -1)
            v = v.reshape(B, S, NH, -1)
            h, state = _mlstm_scan(q, k, v, i_pre, f_pre)
            h_norm = _multihead_norm(h, gamma).reshape(B, S, -1)
            h_out = jax.nn.sigmoid(o_preact) * h_norm
            y = h_out @ Wout.T
            return (y, *state)
        return _reference_tuple_inner(x, Wq, Wk, Wv, Wog, Wig, big, Wfg, bfg, gamma, Wout)[0]

    def _L0_ffn_ref(x, w_gate, w_up, w_down):
        import jax, jax.numpy as jnp
        import numpy as np
        DIM_IN = 512
        DIM_HIDDEN = 2048
        gate = jnp.einsum('bsd,hd->bsh', x, w_gate)
        up = jnp.einsum('bsd,hd->bsh', x, w_up)
        gated = jax.nn.silu(gate) * up
        return jnp.einsum('bsh,dh->bsd', gated, w_down)
    x = L0_attn_x
    xn = _layernorm(x, axis=-1)
    x = x + _L0_attn_ref(xn, L0_attn_Wq, L0_attn_Wk, L0_attn_Wv, L0_attn_Wog, L0_attn_Wig, L0_attn_big, L0_attn_Wfg, L0_attn_bfg, L0_attn_gamma, L0_attn_Wout) + _L0_ffn_ref(xn, L0_ffn_w_gate, L0_ffn_w_up, L0_ffn_w_down)
    return x

_drawn_inputs = setup_inputs


def setup_inputs(seed=0):
    import zlib

    import numpy as np

    out = dict(_drawn_inputs(seed))
    spreads = {'L0_attn_gamma': (1.0, 0.2)}
    factors = {'L0_attn_big': 64.0}
    for name, (base, spread) in spreads.items():
        noise = np.random.default_rng([zlib.crc32(name.encode()), seed]).standard_normal(out[name].shape)
        drawn = base * np.exp(spread * noise) if base else spread * noise
        out[name] = jnp.asarray(drawn.astype(out[name].dtype))
    for name, factor in factors.items():
        out[name] = (out[name] * factor).astype(out[name].dtype)
    return out
```

```python
from contextlib import ExitStack

import concourse.bass as bass
from concourse import mybir

ALU = mybir.AluOpType
ACT = mybir.ActivationFunctionType
AX = mybir.AxisListType
F32 = mybir.dt.float32
F32R = mybir.dt.float32r
F16 = mybir.dt.float16
BF16 = mybir.dt.bfloat16
I32 = mybir.dt.int32
R_MAX = bass.bass_isa.ReduceOp.max

P = 128
D = 512
KC = D // P
BATCH, SEQ = 8, 1024
BLOCK = 256
NCH = BLOCK // P
NB = BATCH * SEQ // BLOCK
PER_SEQ = SEQ // BLOCK
NH, DQ, DV = 8, 32, 64
NG = 2
HG = NH // NG
VW = DV + 2
GW = HG * VW
HID = 2048
NJ = HID // P
GR = 40
NU = 2 * NH * DQ

XS = 2.0 ** 8
WS = 2.0 ** 14
HS = 2.0 ** -50
OS = 2.0 ** 10
MASKED = -30000.0
CAP = 15.0
LN_EPS, EPS = 1e-5, 1e-6

USES = (["gates", "q", "k", "v0", "v1", "ffn0", "ffn1", "ffn2", "ffn3", "wT", "wbc", "ffn4", "kT", "ffn5", "o0",
         "ffn6", "st0", "ffn7", "ffn8", "st1", "ffn9", "ffn10", "st2", "ffn11", "hoT0", "ffn12", "st3", "o1",
         "ffn13", "att0", "ffn14", "ffn15", "xT0", "xT1", "hoT1", "att1"])
NUSE = len(USES)
assert NUSE % 3 == 0
TELLS = [n for n in USES if not n.startswith("xT")]


def bank_no(name):
    return USES.index(name) % 3


def uses_told(b, before=NUSE):
    return sum(n in TELLS for n in USES[b:before:3])


AFTER = {j: [] for j in range(NJ)}
AFTER[2] = ["stats"]
AFTER[3] = ["wT", "wbc"]
AFTER[4] = ["kT", "es0"]
AFTER[5] = ["o0", "mean_var"]
AFTER[6] = ["es1", "pv0"]
AFTER[7] = ["xn"]
AFTER[8] = ["es2", "pv1", "center0"]
AFTER[9] = ["scale0"]
AFTER[10] = ["heads0", "es3", "pv2"]
AFTER[11] = ["hoT0"]
AFTER[12] = ["pv3", "o1", "center1"]
AFTER[13] = ["att0", "scale1"]
AFTER[14] = ["heads1"]
AFTER[15] = ["xT0", "xT1", "hoT1"]

WCOLS = {"gates": KC * GR, "qk": KC * NU, "v": KC * D, "o": KC * D, "g": KC * HID, "u": KC * HID, "d": NJ * D,
         "out": KC * D}
WNAMES = list(WCOLS)
HALF = 8192
ROUNDS = [(1, ["gates", "qk", "v", "o"]), (0, ["g"]), (1, ["u"]), (0, ["d"]), (1, ["out"])]
NS = len(WNAMES)
U_ROUND = 2


START = 1
DVE_OWN = 55


class Count:

    def __init__(self, sem, per):
        self.sem, self.per, self.k = sem, per, 0

    def step(self, ins):
        self.k += 1
        ins.then_inc(self.sem, 1)

    def settle(self, eng, i):
        eng.wait_ge(self.sem, i * self.per + self.k)

    def close(self):
        assert self.k == self.per, (self.k, self.per)


def mlstm_mlp_kernel(nc, x, w_dram, gate_bias, gamma, out):
    ctx = ExitStack()
    with ctx:
        def sb(name, shape, dt):
            return ctx.enter_context(nc.sbuf_tensor(name, shape, dt))

        def pb(name):
            return ctx.enter_context(nc.psum_tensor(name, [P, 512], F32))

        def sem(name):
            return ctx.enter_context(nc.semaphore(name))

        wt = {n: sb(f"parts_{n}", [P, 2, c], F16) for n, c in WCOLS.items()}
        w_gates = wt["gates"][:, :, :].rearrange("p h (k f) -> p h k f", k=KC)
        w_qk = wt["qk"][:, :, :].rearrange("p h (k f) -> p h k f", k=KC)
        w_v = wt["v"][:, :, :].rearrange("p h (k f) -> p h k f", k=KC)
        w_o = wt["o"][:, :, :].rearrange("p h (k f) -> p h k f", k=KC)
        w_g = wt["g"][:, :, :].rearrange("p h (k f) -> p h k f", k=KC)
        w_u = wt["u"][:, :, :].rearrange("p h (k f) -> p h k f", k=KC)
        w_d = wt["d"][:, :, :].rearrange("p h (j f) -> p h j f", j=NJ)
        w_out = wt["out"][:, :, :].rearrange("p h (k f) -> p h k f", k=KC)

        ident = sb("ident", [P, P], F32)
        ident_b = sb("ident_b", [P, P], BF16)
        mask = sb("mask", [P, HG, P], BF16)
        spread = sb("spread", [P, NG, P], F32)
        diag = sb("diag", [P, NH], F32)
        own_head = sb("own_head", [P, GW], F32)
        restart = sb("restart", [NH, BLOCK], F32)
        keep = sb("keep", [P, NB + 1], F32)
        amax = sb("amax", [P, NS], F32)
        amax_all = sb("amax_all", [P, NS], F32)
        pow2 = sb("pow2", [P, NS], F32)
        wscale = sb("wscale", [P, NS], F32)
        unscale = sb("unscale", [P, NS + 2], F32)
        bias = sb("bias", [GR, 1], F32)
        gam = sb("gam", [P, KC], F32)
        half_pow = sb("half_pow", [P, NH], F32)
        begun = sb("begun", [1, 10], F32)
        ln_eps = sb("ln_eps", [P, NCH], F32)
        xs = sb("xs", [P, NCH], F32)
        minus_xs = sb("minus_xs", [P, NCH], F32)
        sc = {n: i for i, n in enumerate(WNAMES)}

        xt = sb("xt", [P, KC, 2, BLOCK], F16)
        pair_r = sb("pair_r", [P, NH, P], F32R)
        pair_l = sb("pair_l", [P, BLOCK], F32R)

        sizes = [("qs", 512), ("qi", 512), ("qb", 2048), ("kf", 512), ("kt", 512), ("v", NCH * NH * VW), ("to", 512),
                 ("pm", 1024), ("tg", 256), ("lf", 256), ("ip", 256), ("bc", 256), ("mm", 256), ("uu", 256),
                 ("aa", 256), ("wr", 256), ("uhl", 256), ("state", NG * GW), ("upd", GW), ("num", NH * VW),
                 ("sq", 512), ("hof", 512), ("hoh", 512), ("tt", 512), ("hh", 768), ("res", 1024), ("wtok", NCH * 72),
                 ("small", 160)]
        first_x = max(sum(n for _, n in sizes), 2 * HALF - 2048)
        cols = first_x + 2048
        arena = sb("arena", [P, cols], F32)
        at, off = {}, 0
        for name, n in sizes:
            at[name] = arena[:, off:off + n]
            off += n
        stage = [arena[:, 0:HALF], arena[:, HALF:2 * HALF]]
        xin = arena[:, first_x:first_x + 1024].rearrange("p (c d) -> p c d", c=NCH)
        xn = arena[:, first_x + 1024:first_x + 2048].rearrange("p (c d) -> p c d", c=NCH)

        qs = at["qs"].rearrange("p (g t) -> p g t", g=NG)
        qi = at["qi"].rearrange("p (g t) -> p g t", g=NG)
        qb = at["qb"].rearrange("p (g h t) -> p g h t", g=NG, h=HG)
        kf = at["kf"].rearrange("p (g t) -> p g t", g=NG)
        kt = at["kt"].rearrange("p (c f) -> p c f", c=NCH)
        v = at["v"].rearrange("p (c h e) -> p c h e", c=NCH, h=NH)
        to = at["to"]
        pm = at["pm"].rearrange("p (b n) -> p b n", b=2)
        tg, lf, ip, bc, mm = (at[n] for n in ("tg", "lf", "ip", "bc", "mm"))
        uu, aa, wr = at["uu"], at["aa"], at["wr"]
        we = at["tg"]
        uhl = at["uhl"].bitcast(F32R)
        a_hi = at["lf"].bitcast(F32R)
        state = at["state"].rearrange("p (g n) -> p g n", g=NG)
        upd = at["upd"]
        num = at["num"].rearrange("p (h e) -> p h e", h=NH)
        sq = at["sq"].rearrange("p (h e) -> p h e", h=NH)
        hof = at["hof"]
        ho = at["hoh"].bitcast(F16).rearrange("p (a k t) -> p a k t", a=2, k=KC)
        tt = at["tt"].rearrange("p (b t) -> p b t", b=2)
        HB = 3
        hh = at["hh"].bitcast(F16).rearrange("p (b a t) -> p b a t", b=HB, a=2)
        res = at["res"].rearrange("p (c d) -> p c d", c=NCH)
        wtok = at["wtok"].rearrange("p (c r) -> p c r", c=NCH)
        small = at["small"]
        bn6 = small[:, 0:12].rearrange("p (c s) -> p c s", c=NCH)
        mean_var = small[:, 12:16].rearrange("p (c s) -> p c s", c=NCH)
        shift, rstd = small[:, 16:18], small[:, 18:20]
        hsum, mu, den, rden, vsum, var, rd, fac = (small[:, 24 + 8 * n:32 + 8 * n] for n in range(8))
        m_carry = small[0:NH, 96:97]
        decay = small[:, 100:100 + NG * NCH].rearrange("p (g c) -> p g c", g=NG)

        work = [pb(f"work{n}") for n in range(3)]
        acc = [pb(f"acc{c}") for c in range(NCH)]
        e_bank, s_bank, o_bank = pb("e_bank"), pb("s_bank"), pb("o_bank")

        w_loaded = [sem(f"w_loaded{n}") for n in range(len(ROUNDS))]
        small_loaded = sem("small_loaded")
        w_max = sem("w_max")
        w_max_all = sem("w_max_all")
        w_scaled = sem("w_scaled")
        w_hi = sem("w_hi")
        w_split = sem("w_split")
        w_unscaled = sem("w_unscaled")
        consts = sem("consts")
        dve_set = sem("dve_set")
        pool_set = sem("pool_set")
        ready_set = sem("ready_set")
        first_xt = sem("first_xt")
        x_loaded = sem("x_loaded")
        out_stored = sem("out_stored")
        res_copied = sem("res_copied")
        res_done = sem("res_done")
        work_full = sem("work_full")
        work_free = [sem(f"work_free{n}") for n in range(3)]
        stats_ready = sem("stats_ready")
        factors_ready = sem("factors_ready")
        xn_ready = sem("xn_ready")
        xt_hi = sem("xt_hi")
        xt_ready = sem("xt_ready")
        log_f_ready = sem("log_f_ready")
        rows_ready = sem("rows_ready")
        we_ready = sem("we_ready")
        parts_ready = sem("parts_ready")
        pair_ready = sem("pair_ready")
        e_full = sem("e_full")
        s_full = sem("s_full")
        exp_done = sem("exp_done")
        p_ready = sem("p_ready")
        qb_ready = sem("qb_ready")
        qi_ready = sem("qi_ready")
        pv_full = sem("pv_full")
        num_ready = sem("num_ready")
        state_ready = sem("state_ready")
        centered = sem("centered")
        squared = sem("squared")
        var_ready = sem("var_ready")
        rd_ready = sem("rd_ready")
        ho_ready = sem("ho_ready")
        ho_hi = sem("ho_hi")
        tanh_done = sem("tanh_done")
        h_hi = sem("h_hi")
        h_ready = sem("h_ready")
        acc_full = sem("acc_full")
        acc_free = sem("acc_free")
        act_own = sem("act_own")
        dve_own = sem("dve_own")
        pool_own = sem("pool_own")

        def bank(name):
            return work[bank_no(name)]

        def free_of(name):
            return work_free[bank_no(name)]

        def wait_bank(eng, i, name):
            n, b = USES.index(name), bank_no(name)
            eng.wait_ge(work_free[b], START + i * uses_told(b) + uses_told(b, n))
            if n >= 3 and USES[n - 3].startswith("xT"):
                eng.wait_ge(xt_ready, NCH * (i + 1) + int(USES[n - 3][-1]) + 1)

        def wait_full(eng, i, name):
            eng.wait_ge(work_full, i * NUSE + USES.index(name) + 1)

        def wait_drained(eng, i, name):
            b = bank_no(name)
            eng.wait_ge(work_free[b], START + i * uses_told(b) + uses_told(b, USES.index(name)) + 1)

        block = ctx.enter_context(nc.Block())
        x_blocks = x.rearrange("(i c p) d -> i p c d", c=NCH, p=P)
        out_blocks = out.rearrange("(i c p) d -> i p c d", c=NCH, p=P)

        @block.sync
        def _(sp):
            sp.dma_start(bias[:, :], gate_bias).then_inc(small_loaded, 16)
            sp.dma_start(gam[:, :], gamma).then_inc(small_loaded, 16)
            for r, (half, names) in enumerate(ROUNDS):
                if r >= 2:
                    sp.wait_ge(w_split, sum(len(n) for _, n in ROUNDS[:r - 1]))
                o = 0
                for n in names:
                    sp.dma_start(stage[half][:, o:o + WCOLS[n]], w_dram[n]).then_inc(w_loaded[r], 16)
                    o += WCOLS[n]
            sp.wait_ge(w_split, sum(len(n) for _, n in ROUNDS[:U_ROUND + 1]))
            sp.dma_start(xin, x_blocks[0, :, :, :]).then_inc(x_loaded, 16)
            with sp.Fori(0, NB) as i:
                sp.wait_ge(res_copied, NCH * (i + 1))
                sp.dma_start(xin, x_blocks[bass.ds((i + 1) % NB, 1), :, :, :]).then_inc(x_loaded, 16)
                sp.wait_ge(res_done, START + NCH * (i + 1))
                sp.dma_start(out_blocks[bass.ds(i, 1), :, :, :], res).then_inc(out_stored, 16)
            sp.wait_ge(x_loaded, 16 * (NB + 1))
            sp.wait_ge(out_stored, START + 16 * NB)

        @block.gpsimd
        def _(pool):
            g = nc.gpsimd
            own_k = [0]

            def link(ins):
                own_k[0] += 1
                ins.then_inc(pool_set, 1)
                pool.wait_ge(pool_set, own_k[0])

            link(g.memset(ident[:, :], 0.0))
            link(g.affine_select(out=ident[:, :], in_=ident[:, :], compare_op=ALU.not_equal, fill=1.0, base=0,
                                 pattern=[[-1, P]], channel_multiplier=1))
            link(g.tensor_copy(ident_b[:, :], ident[:, :]))
            link(g.memset(mask[:, :, :], 0.0))
            link(g.affine_select(out=mask[:, :, :], in_=mask[:, :, :], compare_op=ALU.is_ge, fill=MASKED, base=0,
                                 pattern=[[0, HG], [1, P]], channel_multiplier=-1))
            link(g.memset(spread[:, :, :], 0.0))
            spread4 = spread[:, :, :].rearrange("p g (h d) -> p g h d", h=HG)
            link(g.affine_select(out=spread4, in_=spread4, compare_op=ALU.not_equal, fill=1.0, base=0,
                                 pattern=[[-HG, NG], [-1, HG], [0, DQ]], channel_multiplier=1))
            link(g.memset(diag[:, :], 0.0))
            for first in (0, 32):
                link(g.affine_select(out=diag[:, :], in_=diag[:, :], compare_op=ALU.not_equal, fill=1.0, base=-first,
                                     pattern=[[-1, NH]], channel_multiplier=1))
            link(g.memset(pair_r[:, :, :].bitcast(F32), 0.0))
            for first in (64, 96):
                link(g.affine_select(out=pair_r[:, :, :], in_=pair_r[:, :, :].bitcast(F32),
                                     compare_op=ALU.not_equal, fill=1.0, base=-first,
                                     pattern=[[-1, NH], [0, P]], channel_multiplier=1))
            link(g.memset(pair_l[:, :].bitcast(F32), 0.0))
            link(g.memset(pair_l[0:NH, :].bitcast(F32), -1.0))
            link(g.memset(pair_l[32:32 + NH, :].bitcast(F32), -1.0))
            link(g.memset(own_head[:, :], 0.0))
            for h in range(HG):
                link(g.memset(own_head[h * DQ:(h + 1) * DQ, h * VW:(h + 1) * VW], 1.0))
            link(g.memset(restart[:, :], 1.0))
            link(g.memset(restart[:, 0:BLOCK:P], 0.0))
            link(g.memset(keep[:, :], 1.0))
            link(g.memset(keep[:, 0:NB + 1:PER_SEQ], 0.0))
            link(g.memset(ln_eps[:, :], LN_EPS))
            link(g.memset(xs[:, :], XS))
            link(g.memset(minus_xs[:, :], -XS))
            g.memset(half_pow[:, :], -0.5).then_inc(consts, 1)
            done = 0
            for _, names in ROUNDS:
                a, b = sc[names[0]], sc[names[-1]] + 1
                done += len(names)
                pool.wait_ge(w_max, done)
                g.partition_all_reduce(amax_all[:, a:b], amax[:, a:b], P, R_MAX).then_inc(w_max_all, 1)
            pool.wait_ge(w_split, NS)
            link(g.memset(wr, 0.0))
            link(g.memset(tg, 0.0))
            link(g.memset(uhl.bitcast(F32), 0.0))
            link(g.memset(at["state"], 0.0))
            link(g.memset(at["qb"], 0.0))
            link(g.memset(v[:, :, :, DV:DV + 1], 1.0))
            link(g.memset(v[:, :, :, DV + 1:VW], 0.0))
            for n, started in enumerate((*work_free, out_stored, res_done, exp_done, p_ready, num_ready, ho_ready,
                                         state_ready)):
                g.memset(begun[0:1, n:n + 1], 0.0).then_inc(started, START)
            g.memset(small, 0.0).then_inc(ready_set, 1)
            pool.wait_ge(ready_set, 1)

            def norm_factors(i, own):
                own.step(g.tensor_tensor(rstd, mean_var[:, :, 1], ln_eps[:, :], ALU.add))
                own.settle(pool, i)
                own.step(g.tensor_tensor(rstd, rstd, half_pow[:, 0:NCH], ALU.pow))
                own.settle(pool, i)
                own.step(g.tensor_tensor(shift, rstd, minus_xs[:, :], ALU.mult))
                own.settle(pool, i)
                own.step(g.tensor_tensor(rstd, rstd, xs[:, :], ALU.mult))
                g.tensor_tensor(shift, shift, mean_var[:, :, 0], ALU.mult).then_inc(factors_ready, 1)

            pool.wait_ge(stats_ready, 2)
            first = Count(pool_set, 0)
            first.k = own_k[0]
            norm_factors(0, first)

            with pool.Fori(0, NB) as i:
                own = Count(pool_own, 4)
                def pair(c):
                    g.tensor_tensor(pair_r[0:GR, :, :],
                                    uhl[0:GR, c * P:(c + 1) * P].bitcast(F32).unsqueeze(1).broadcast_to((GR, NH, P)),
                                    diag[0:GR, :].unsqueeze(2).broadcast_to((GR, NH, P)),
                                    ALU.mult).then_inc(pair_ready, 1)

                pool.wait_ge(parts_ready, i + 1)
                pair(0)
                for j in range(NJ):
                    pool.wait_ge(h_hi, i * NJ + j + 1)
                    g.tensor_tensor(hh[:, j % HB, 1, :], tt[:, j % 2, :], hh[:, j % HB, 0, :],
                                    ALU.subtract).then_inc(h_ready, 1)
                    for step in AFTER[j]:
                        if step == "es1":
                            pool.wait_ge(e_full, i * 4 + 2)
                            pair(1)
                        if step.startswith("scale"):
                            pool.wait_ge(var_ready, i * NCH + int(step[-1]) + 1)
                            g.tensor_tensor(rd, var, half_pow[:, :], ALU.pow).then_inc(rd_ready, 1)
                        if step == "mean_var":
                            pool.wait_ge(stats_ready, NCH * (i + 2))
                            norm_factors(i, own)
                own.close()

        @block.scalar
        def _(act):
            s = nc.scalar
            n = 0
            for r, (half, names) in enumerate(ROUNDS):
                o = 0
                for name in names:
                    n += 1
                    act.wait_ge(w_scaled, r + 1)
                    s.activation(wt[name][:, 0, :], stage[half][:, o:o + WCOLS[name]], ACT.Copy,
                                 scale=wscale[:, sc[name]:sc[name] + 1]).then_inc(w_hi, 1)
                    o += WCOLS[name]

            def x_high(i, c, src):
                s.activation(xt[:, :, 0, c * P:(c + 1) * P], src.rearrange("p (k t) -> p k t", k=KC),
                             ACT.Copy).then_inc(xt_hi, 1)

            def norm_x(i):
                act.wait_ge(factors_ready, i + 1)
                for c in range(NCH):
                    s.activation(xn[:, c, :], xin[:, c, :], ACT.Identity, bias=shift[:, c:c + 1],
                                 scale=rstd[:, c:c + 1]).then_inc(xn_ready, 1)

            act.wait_ge(w_unscaled, 1)
            act.wait_ge(ready_set, 1)
            norm_x(0)
            for c in range(NCH):
                act.wait_ge(first_xt, c + 1)
                x_high(0, c, (e_bank, s_bank)[c][:, :])

            with act.Fori(0, NB) as i:
                own = Count(act_own, 1)
                wait_full(act, i, "gates")
                s.activation(tg[0:GR, :], bank("gates")[0:GR, 0:BLOCK], ACT.Tanh, bias=bias[:, 0:1],
                             scale=unscale[0:GR, 0:1]).then_inc(free_of("gates"), 1)
                wait_drained(act, i, "gates")
                own.step(s.activation(lf[0:NH, :], tg[32:32 + NH, :], ACT.Exp, scale=-CAP))
                own.settle(act, i)
                s.activation(lf[0:NH, :], lf[0:NH, :], ACT.Ln, bias=1.0).then_inc(log_f_ready, 1)
                wait_full(act, i, "q")
                s.activation(at["qs"], bank("q")[:, :], ACT.Copy,
                             scale=unscale[:, NS:NS + 1]).then_inc(free_of("q"), 1)
                wait_full(act, i, "k")
                s.activation(at["kf"], bank("k")[:, :], ACT.Copy,
                             scale=unscale[:, sc["qk"]:sc["qk"] + 1]).then_inc(free_of("k"), 1)
                for c in range(NCH):
                    wait_full(act, i, f"v{c}")
                    s.activation(v[:, c, :, 0:DV], bank(f"v{c}")[:, :].rearrange("p (h e) -> p h e", h=NH), ACT.Copy,
                                 scale=unscale[:, sc["v"]:sc["v"] + 1]).then_inc(free_of(f"v{c}"), 1)
                act.wait_ge(out_stored, START + 16 * i)
                act.wait_ge(x_loaded, 16 * (i + 1))
                for c in range(NCH):
                    s.activation(res[:, c, :], xin[:, c, :], ACT.Copy).then_inc(res_copied, 1)
                for j in range(NJ):
                    wait_full(act, i, f"ffn{j}")
                    if j >= 2:
                        act.wait_ge(h_ready, i * NJ + j - 1)
                    s.activation(tt[:, j % 2, :], bank(f"ffn{j}")[:, 0:BLOCK], ACT.Tanh,
                                 scale=unscale[:, sc["g"]:sc["g"] + 1]).then_inc(tanh_done, 1)
                    wait_drained(act, i, f"ffn{j}")
                    s.activation(hh[:, j % HB, 0, :], tt[:, j % 2, :], ACT.Copy).then_inc(h_hi, 1)
                    if j == 2:
                        act.wait_ge(rows_ready, i + 1)
                        s.activation(we[0:72, :], wr[0:72, :], ACT.Exp).then_inc(we_ready, 1)
                    for step in AFTER[j]:
                        k = int(step[-1]) if step[-1].isdigit() else 0
                        if step == "wT":
                            wait_full(act, i, "wT")
                            s.activation(at["wtok"], bank("wT")[:, 0:NCH * 72], ACT.Copy).then_inc(free_of("wT"), 1)
                        elif step.startswith("es"):
                            act.wait_ge(e_full, i * 4 + k + 1)
                            if k >= 2:
                                act.wait_ge(pv_full, i * 4 + k - 1)
                            s.activation(pm[:, k % 2, :], e_bank[:, :], ACT.Exp).then_inc(exp_done, 1)
                        elif step in ("o0", "o1"):
                            wait_full(act, i, step)
                            act.wait_ge(ho_ready, START + i * NCH + k)
                            s.activation(to, bank(step)[:, :], ACT.Tanh,
                                         scale=unscale[:, sc["o"]:sc["o"] + 1]).then_inc(free_of(step), 1)
                        elif step.startswith("pv"):
                            act.wait_ge(pv_full, i * 4 + k + 1)
                            act.wait_ge(ho_ready, START + i * NCH + k // 2)
                            s.activation(num[:, HG * (k % 2):HG * (k % 2) + HG, :],
                                         o_bank[:, 0:GW].rearrange("p (h e) -> p h e", h=HG),
                                         ACT.Copy).then_inc(num_ready, 1)
                        elif step.startswith("center"):
                            act.wait_ge(centered, i * NCH + k + 1)
                            s.activation(sq, num[:, :, 0:DV], ACT.Square).then_inc(squared, 1)
                        elif step.startswith("hoT"):
                            wait_full(act, i, step)
                            s.activation(ho[:, 0, :, :], bank(step)[:, :].rearrange("p (k t) -> p k t", k=KC),
                                         ACT.Copy).then_inc(ho_hi, 1)
                        elif step == "xn":
                            act.wait_ge(xt_ready, NCH * (i + 1))
                            norm_x(i + 1)
                        elif step.startswith("xT"):
                            wait_full(act, i, step)
                            x_high(i, k, bank(step)[:, :])
                own.close()

        @block.vector
        def _(dve):
            d = nc.vector
            k = [0]

            def link(ins):
                k[0] += 1
                ins.then_inc(dve_set, 1)
                dve.wait_ge(dve_set, k[0])

            def maxima(r):
                half, names = ROUNDS[r]
                dve.wait_ge(w_loaded[r], 16 * len(names))
                o = 0
                for name in names:
                    w = stage[half][:, o:o + WCOLS[name]]
                    if name == "out":
                        dve.wait_ge(small_loaded, 32)
                        for c in range(KC):
                            link(d.tensor_scalar(w[:, c * D:(c + 1) * D], w[:, c * D:(c + 1) * D], gam[:, c:c + 1],
                                                 None, ALU.mult))
                    d.tensor_reduce(amax[:, sc[name]:sc[name] + 1], w, AX.X, ALU.max,
                                    apply_absolute_value=True).then_inc(w_max, 1)
                    o += WCOLS[name]

            def split(r, done):
                half, names = ROUNDS[r]
                a, b = sc[names[0]], sc[names[-1]] + 1
                dve.wait_ge(w_max_all, r + 1)
                link(d.tensor_scalar(amax_all[:, a:b], amax_all[:, a:b], 1e-30, None, ALU.max))
                link(d.tensor_scalar(pow2[:, a:b].bitcast(I32), amax_all[:, a:b].bitcast(I32), 0x7F800000, None,
                                     ALU.bitwise_and))
                link(d.reciprocal(wscale[:, a:b], pow2[:, a:b]))
                d.tensor_scalar(wscale[:, a:b], wscale[:, a:b], WS, None, ALU.mult).then_inc(w_scaled, 1)
                dve.wait_ge(w_scaled, r + 1)
                o = 0
                for n, name in enumerate(names):
                    dve.wait_ge(w_hi, done + n + 1)
                    d.scalar_tensor_tensor(out=wt[name][:, 1, :], in0=stage[half][:, o:o + WCOLS[name]],
                                           scalar=wscale[:, sc[name]:sc[name] + 1], in1=wt[name][:, 0, :],
                                           op0=ALU.mult, op1=ALU.subtract).then_inc(w_split, 1)
                    o += WCOLS[name]

            maxima(0)
            done = 0
            for r in range(len(ROUNDS)):
                split(r, done)
                done += len(ROUNDS[r][1])
                if r + 1 < len(ROUNDS):
                    maxima(r + 1)

            back = 1.0 / (XS * WS)
            for name, f in (("gates", back / CAP), ("qk", back), ("v", back), ("o", back / 2), ("g", back / 2),
                            ("out", 1.0 / (WS * OS * 2))):
                link(d.tensor_scalar(unscale[:, sc[name]:sc[name] + 1], pow2[:, sc[name]:sc[name] + 1], f, None,
                                     ALU.mult))
            link(d.tensor_scalar(unscale[:, NS:NS + 1], unscale[:, sc["qk"]:sc["qk"] + 1], float(DQ) ** -0.5, None,
                                 ALU.mult))
            link(d.tensor_tensor(unscale[:, NS + 1:NS + 2], pow2[:, sc["g"]:sc["g"] + 1],
                                 pow2[:, sc["u"]:sc["u"] + 1], ALU.mult))
            link(d.tensor_tensor(unscale[:, NS + 1:NS + 2], unscale[:, NS + 1:NS + 2],
                                 pow2[:, sc["d"]:sc["d"] + 1], ALU.mult))
            link(d.tensor_scalar(unscale[:, NS + 1:NS + 2], unscale[:, NS + 1:NS + 2], 2.0 ** 5 / WS, None, ALU.mult))
            dve.wait_ge(small_loaded, 32)
            d.tensor_scalar(bias[:, :], bias[:, :], 1.0 / CAP, None, ALU.mult).then_inc(w_unscaled, 1)

            def stats(own):
                for c in range(NCH):
                    own.step(d.bn_stats(bn6[:, c, :], xin[:, c, :]))

            def means():
                for c in range(NCH):
                    d.bn_aggr(mean_var[:, c, :], bn6[:, c, :]).then_inc(stats_ready, 1)

            def x_low(i, c, src):
                dve.wait_ge(xt_hi, NCH * i + c + 1)
                d.tensor_tensor(xt[:, :, 1, c * P:(c + 1) * P], src.rearrange("p (k t) -> p k t", k=KC),
                                xt[:, :, 0, c * P:(c + 1) * P], ALU.subtract).then_inc(xt_ready, 1)

            dve.wait_ge(x_loaded, 16)
            dve.wait_ge(ready_set, 1)
            first = Count(dve_set, 0)
            first.k = k[0]
            stats(first)
            first.settle(dve, 0)
            means()
            for c in range(NCH):
                x_low(0, c, (e_bank, s_bank)[c][:, :])

            def add_mlstm(i, c):
                wait_full(dve, i, f"att{c}")
                dve.wait_ge(res_copied, i * NCH + c + 1)
                d.scalar_tensor_tensor(out=res[:, c, :], in0=bank(f"att{c}")[:, :],
                                       scalar=unscale[:, sc["out"]:sc["out"] + 1], in1=res[:, c, :],
                                       op0=ALU.mult, op1=ALU.add).then_inc(free_of(f"att{c}"), 1)

            with dve.Fori(0, NB) as i:
                own = Count(dve_own, DVE_OWN)

                dve.wait_ge(log_f_ready, i + 1)
                own.step(d.tensor_scalar(lf[0:NH, :], lf[0:NH, :], -1.0, None, ALU.mult))
                own.step(d.tensor_scalar(ip[0:NH, :], tg[0:NH, :], CAP, None, ALU.mult))
                own.settle(dve, i)
                own.step(d.tensor_tensor_scan(bc[0:NH, :], restart[:, :], lf[0:NH, :], 0.0, ALU.mult, ALU.add))
                own.step(d.tensor_tensor_scan(mm[0:NH, :], lf[0:NH, :], ip[0:NH, :], m_carry, ALU.add, ALU.max))
                own.settle(dve, i)
                own.step(d.tensor_tensor(uu[0:NH, :], mm[0:NH, :], bc[0:NH, :], ALU.subtract))
                own.step(d.tensor_tensor(aa[0:NH, :], ip[0:NH, :], bc[0:NH, :], ALU.subtract))
                own.settle(dve, i)
                for c in range(NCH):
                    span, end = slice(c * P, (c + 1) * P), c * P + P - 1
                    prev = m_carry if c == 0 else mm[0:NH, c * P - 1:c * P]
                    own.step(d.tensor_scalar(wr[0:NH, span], uu[0:NH, span], prev, -1.0, ALU.subtract, ALU.mult))
                    own.step(d.tensor_scalar(wr[32:32 + NH, span], aa[0:NH, span], uu[0:NH, end:end + 1], None,
                                             ALU.subtract))
                d.tensor_scalar(wr[64:64 + NH, :], mm[0:NH, :], -1.0, None, ALU.mult).then_inc(rows_ready, 1)
                own.step(d.tensor_copy(uhl[0:NH, :], uu[0:NH, :]))
                own.step(d.tensor_copy(a_hi[0:NH, :], aa[0:NH, :]))
                own.step(d.tensor_copy(pair_l[64:64 + NH, :], aa[0:NH, :]))
                own.settle(dve, i)
                own.step(d.tensor_scalar(m_carry, mm[0:NH, BLOCK - 1:BLOCK], keep[0:NH, bass.ds(i + 1, 1)], None,
                                         ALU.mult))
                own.step(d.tensor_tensor(uhl[32:32 + NH, :], uu[0:NH, :], uhl[0:NH, :].bitcast(F32), ALU.subtract))
                d.tensor_tensor(pair_l[96:96 + NH, :], aa[0:NH, :], a_hi[0:NH, :].bitcast(F32),
                                ALU.subtract).then_inc(parts_ready, 1)
                wait_drained(dve, i, "q")
                for h in range(HG):
                    rows = slice(h * DQ, (h + 1) * DQ)
                    d.tensor_copy(qb[rows, :, h, :], qs[rows, :, :]).then_inc(qb_ready, 1)

                for j in range(NJ):
                    b = bank(f"ffn{j}")
                    dve.wait_ge(tanh_done, i * NJ + j + 1)
                    own.step(d.scalar_tensor_tensor(out=tt[:, j % 2, :], in0=tt[:, j % 2, :], scalar=1.0,
                                                    in1=b[:, 0:BLOCK], op0=ALU.add, op1=ALU.mult))
                    own.settle(dve, i)
                    d.scalar_tensor_tensor(out=tt[:, j % 2, :], in0=tt[:, j % 2, :], scalar=HS,
                                           in1=b[:, BLOCK:2 * BLOCK], op0=ALU.mult,
                                           op1=ALU.mult).then_inc(free_of(f"ffn{j}"), 1)
                    for step in AFTER[j]:
                        k_ = int(step[-1]) if step[-1].isdigit() else 0
                        if step == "stats":
                            dve.wait_ge(x_loaded, 16 * (i + 2))
                            stats(own)
                        elif step == "mean_var":
                            means()
                        elif step == "wbc":
                            wb = bank("wbc")[:, :].rearrange("p (g t) -> p g t", g=NG)
                            wait_full(dve, i, "wbc")
                            wait_drained(dve, i, "q")
                            d.tensor_tensor(at["qi"], at["qs"], bank("wbc")[:, :], ALU.mult).then_inc(qi_ready, 1)
                            d.tensor_copy(decay, wb[:, :, P - 1:BLOCK:P]).then_inc(free_of("wbc"), 1)
                        elif step == "kT":
                            wait_full(dve, i, "kT")
                            wait_drained(dve, i, "wT")
                            d.tensor_tensor(kt[:, :, :].rearrange("p c (h e) -> p c h e", h=NH),
                                            bank("kT")[:, :].rearrange("p (c h e) -> p c h e", c=NCH, h=NH),
                                            wtok[:, :, 32:32 + NH].unsqueeze(3).broadcast_to((P, NCH, NH, DQ)),
                                            ALU.mult).then_inc(free_of("kT"), 1)
                        elif step.startswith("es"):
                            dve.wait_ge(exp_done, START + i * 4 + k_ + 1)
                            dve.wait_ge(s_full, i * 4 + k_ + 1)
                            d.tensor_tensor(pm[:, k_ % 2, :], pm[:, k_ % 2, :], s_bank[:, :],
                                            ALU.mult).then_inc(p_ready, 1)
                        elif step.startswith("pv"):
                            c, g = k_ // 2, k_ % 2
                            wait_full(dve, i, f"st{k_}")
                            wait_drained(dve, i, "wbc")
                            d.tensor_tensor(upd, own_head[:, :], bank(f"st{k_}")[:, 0:GW],
                                            ALU.mult).then_inc(free_of(f"st{k_}"), 1)
                            wait_drained(dve, i, f"st{k_}")
                            d.scalar_tensor_tensor(out=state[:, g, :], in0=state[:, g, :],
                                                   scalar=decay[:, g, c:c + 1], in1=upd, op0=ALU.mult,
                                                   op1=ALU.add).then_inc(state_ready, 1)
                            if k_ == 3:
                                dve.wait_ge(state_ready, START + i * 5 + 4)
                                d.tensor_scalar(at["state"], at["state"], keep[:, bass.ds(i + 1, 1)], None,
                                                ALU.mult).then_inc(state_ready, 1)
                        elif step.startswith("center"):
                            dve.wait_ge(num_ready, START + i * 4 + 2 * k_ + 2)
                            own.step(d.tensor_reduce(hsum, num[:, :, 0:DV], AX.X, ALU.add))
                            own.settle(dve, i)
                            own.step(d.tensor_scalar(mu, hsum, 1.0 / DV, None, ALU.mult))
                            own.settle(dve, i)
                            d.tensor_tensor(num[:, :, 0:DV], num[:, :, 0:DV],
                                            mu.unsqueeze(2).broadcast_to((P, NH, DV)),
                                            ALU.subtract).then_inc(centered, 1)
                            own.step(d.scalar_tensor_tensor(out=den, in0=num[:, :, DV], scalar=-1.0,
                                                            in1=wtok[:, k_, 64:64 + NH], op0=ALU.mult, op1=ALU.max))
                            own.settle(dve, i)
                            own.step(d.tensor_tensor(den, den, num[:, :, DV], ALU.max))
                            own.settle(dve, i)
                            own.step(d.tensor_scalar(den, den, EPS, None, ALU.add))
                            own.settle(dve, i)
                            own.step(d.reciprocal(rden, den))
                        elif step.startswith("scale"):
                            dve.wait_ge(squared, i * NCH + k_ + 1)
                            own.step(d.tensor_reduce(vsum, sq, AX.X, ALU.add))
                            own.settle(dve, i)
                            own.step(d.tensor_tensor(vsum, vsum, rden, ALU.mult))
                            own.settle(dve, i)
                            own.step(d.tensor_tensor(vsum, vsum, rden, ALU.mult))
                            own.settle(dve, i)
                            d.tensor_scalar(var, vsum, 1.0 / DV, EPS, ALU.mult, ALU.add).then_inc(var_ready, 1)
                        elif step.startswith("heads"):
                            dve.wait_ge(rd_ready, i * NCH + k_ + 1)
                            own.step(d.scalar_tensor_tensor(out=fac, in0=rden, scalar=OS, in1=rd, op0=ALU.mult,
                                                            op1=ALU.mult))
                            own.settle(dve, i)
                            own.step(d.tensor_tensor(num[:, :, 0:DV], num[:, :, 0:DV],
                                                     fac.unsqueeze(2).broadcast_to((P, NH, DV)), ALU.mult))
                            own.settle(dve, i)
                            wait_drained(dve, i, f"o{k_}")
                            d.scalar_tensor_tensor(out=hof.rearrange("p (h e) -> p h e", h=NH),
                                                   in0=to.rearrange("p (h e) -> p h e", h=NH), scalar=1.0,
                                                   in1=num[:, :, 0:DV], op0=ALU.add,
                                                   op1=ALU.mult).then_inc(ho_ready, 1)
                        elif step.startswith("hoT"):
                            dve.wait_ge(ho_hi, i * NCH + k_ + 1)
                            d.tensor_tensor(ho[:, 1, :, :], bank(step)[:, :].rearrange("p (k t) -> p k t", k=KC),
                                            ho[:, 0, :, :], ALU.subtract).then_inc(free_of(step), 1)
                        elif step.startswith("xT"):
                            x_low(i + 1, k_, bank(step)[:, :])
                        elif step == "att0":
                            add_mlstm(i, 0)
                add_mlstm(i, 1)
                for c in range(NCH):
                    dve.wait_ge(acc_full, i * NCH + c + 1)
                    wait_drained(dve, i, f"att{c}")
                    d.scalar_tensor_tensor(out=res[:, c, :], in0=acc[c][:, :], scalar=unscale[:, NS + 1:NS + 2],
                                           in1=res[:, c, :], op0=ALU.mult, op1=ALU.add).then_inc(res_done, 1)
                own.close()

        @block.tensor
        def _(pe):
            t = nc.tensor

            def three(dst, w, a, first, last):
                t.matmul(dst, w[0], a[0], start=first, stop=False, skip_group_check=True)
                t.matmul(dst, w[0], a[1], start=False, stop=False, skip_group_check=True)
                return t.matmul(dst, w[1], a[0], start=False, stop=last, skip_group_check=True)

            def by_feature(dst, w, f0, f1):
                for k in range(KC):
                    mm_ = three(dst, (w[:, 0, k, f0:f1], w[:, 1, k, f0:f1]), (xt[:, k, 0, :], xt[:, k, 1, :]),
                                k == 0, k == KC - 1)
                return mm_

            def by_token(dst, c, w):
                span = slice(c * P, (c + 1) * P)
                for k in range(KC):
                    mm_ = three(dst, (xt[:, k, 0, span], xt[:, k, 1, span]), (w[:, 0, k, :], w[:, 1, k, :]),
                                k == 0, k == KC - 1)
                return mm_

            pe.wait_ge(consts, 1)
            for c in range(NCH):
                pe.wait_ge(xn_ready, c + 1)
                for k in range(KC):
                    tr = t.transpose((e_bank, s_bank)[c][:, k * P:(k + 1) * P], xn[:, c, k * P:(k + 1) * P],
                                     ident[:, :])
                tr.then_inc(first_xt, 1)

            with pe.Fori(0, NB) as i:
                def down(j):
                    pe.wait_ge(h_ready, i * NJ + j + 1)
                    for c in range(NCH):
                        if j == 0:
                            pe.wait_ge(res_done, START + i * NCH)
                        span = slice(c * P, (c + 1) * P)
                        h = hh[:, j % HB, :, :]
                        mm_ = three(acc[c][:, :], (h[:, 0, span], h[:, 1, span]), (w_d[:, 0, j, :], w_d[:, 1, j, :]),
                                    j == 0, j == NJ - 1)
                        if j == NJ - 1:
                            mm_.then_inc(acc_full, 1)

                def project(c):
                    wait_drained(pe, i, f"hoT{c}")
                    for n in range(KC):
                        mm_ = three(bank(f"att{c}")[:, :], (ho[:, 0, n, :], ho[:, 1, n, :]),
                                    (w_out[:, 0, n, :], w_out[:, 1, n, :]), n == 0, n == KC - 1)
                    mm_.then_inc(work_full, 1)

                pe.wait_ge(xt_ready, NCH * (i + 1))
                wait_bank(pe, i, "gates")
                by_feature(bank("gates")[0:GR, 0:BLOCK], w_gates, 0, GR).then_inc(work_full, 1)
                for name, f in (("q", 0), ("k", NH * DQ)):
                    wait_bank(pe, i, name)
                    for g in range(NG):
                        mm_ = by_feature(bank(name)[:, g * BLOCK:(g + 1) * BLOCK], w_qk, f + g * P, f + (g + 1) * P)
                    mm_.then_inc(work_full, 1)
                for c in range(NCH):
                    wait_bank(pe, i, f"v{c}")
                    by_token(bank(f"v{c}")[:, :], c, w_v).then_inc(work_full, 1)

                for j in range(NJ):
                    name = f"ffn{j}"
                    wait_bank(pe, i, name)
                    by_feature(bank(name)[:, 0:BLOCK], w_g, j * P, (j + 1) * P)
                    by_feature(bank(name)[:, BLOCK:2 * BLOCK], w_u, j * P, (j + 1) * P).then_inc(work_full, 1)
                    if j >= 2:
                        down(j - 2)
                    for step in AFTER[j]:
                        k = int(step[-1]) if step[-1].isdigit() else 0
                        if step in USES:
                            wait_bank(pe, i, step)
                        if step == "wT":
                            pe.wait_ge(we_ready, i + 1)
                            for c in range(NCH):
                                tr = t.transpose(bank(step)[:, c * 72:(c + 1) * 72], we[0:72, c * P:(c + 1) * P],
                                                 ident[0:72, 0:72])
                            tr.then_inc(work_full, 1)
                        elif step == "wbc":
                            for g in range(NG):
                                mm_ = t.matmul(bank(step)[:, g * BLOCK:(g + 1) * BLOCK], spread[0:72, g, :],
                                               we[0:72, :], start=True, stop=True)
                            mm_.then_inc(work_full, 1)
                        elif step == "kT":
                            wait_drained(pe, i, "k")
                            for c in range(NCH):
                                for g in range(NG):
                                    n = c * NG + g
                                    tr = t.transpose(bank(step)[:, n * P:(n + 1) * P], kf[:, g, c * P:(c + 1) * P],
                                                     ident[:, :])
                            tr.then_inc(work_full, 1)
                        elif step.startswith("es"):
                            c, g = k // 2, k % 2
                            span = slice(c * P, (c + 1) * P)
                            pe.wait_ge(pair_ready, i * NCH + c + 1)
                            pe.wait_ge(exp_done, START + i * 4 + k)
                            t.matmul(e_bank[:, :], ident_b[:, :], mask[:, :, :], start=True, stop=False)
                            t.matmul(e_bank[:, :], pair_l[:, span], pair_r[:, g * HG:(g + 1) * HG, :], start=False,
                                     stop=True).then_inc(e_full, 1)
                            pe.wait_ge(qb_ready, (i + 1) * HG)
                            pe.wait_ge(p_ready, START + i * 4 + k)
                            t.matmul(s_bank[:, :], kf[:, g, span], qb[:, g, :, span], start=True,
                                     stop=True).then_inc(s_full, 1)
                        elif step in ("o0", "o1"):
                            by_token(bank(step)[:, :], k, w_o).then_inc(work_full, 1)
                        elif step.startswith("pv"):
                            c, g = k // 2, k % 2
                            span = slice(c * P, (c + 1) * P)
                            pe.wait_ge(qi_ready, i + 1)
                            pe.wait_ge(state_ready, START + i * 5 + (k - 1 if c else 0))
                            pe.wait_ge(num_ready, START + i * 4 + k)
                            t.matmul(o_bank[:, 0:GW], qi[:, g, span], state[:, g, :], start=True, stop=False,
                                     skip_group_check=True)
                            wait_drained(pe, i, f"v{c}")
                            pe.wait_ge(p_ready, START + i * 4 + k + 1)
                            for h in range(HG):
                                mm_ = t.matmul(o_bank[:, h * VW:(h + 1) * VW], pm[:, k % 2, h * P:(h + 1) * P],
                                               v[:, c, g * HG + h, :], start=False, stop=(h == HG - 1),
                                               skip_group_check=True)
                            mm_.then_inc(pv_full, 1)
                            wait_bank(pe, i, f"st{k}")
                            wait_drained(pe, i, "kT")
                            t.matmul(bank(f"st{k}")[:, 0:GW], kt[:, c, g * P:(g + 1) * P],
                                     v[:, c, g * HG:(g + 1) * HG, :], start=True,
                                     stop=True).then_inc(work_full, 1)
                        elif step.startswith("hoT"):
                            pe.wait_ge(ho_ready, START + i * NCH + k + 1)
                            for n in range(KC):
                                tr = t.transpose(bank(step)[:, n * P:(n + 1) * P], hof[:, n * P:(n + 1) * P],
                                                 ident[:, :])
                            tr.then_inc(work_full, 1)
                        elif step == "att0":
                            project(0)
                        elif step.startswith("xT"):
                            pe.wait_ge(xn_ready, NCH * (i + 1) + k + 1)
                            for n in range(KC):
                                tr = t.transpose(bank(step)[:, n * P:(n + 1) * P], xn[:, k, n * P:(n + 1) * P],
                                                 ident[:, :])
                            tr.then_inc(work_full, 1)
                down(NJ - 2)
                down(NJ - 1)
                wait_bank(pe, i, "att1")
                project(1)


def kernel(L0_attn_x, L0_attn_Wq, L0_attn_Wk, L0_attn_Wv, L0_attn_Wog, L0_attn_Wig, L0_attn_big, L0_attn_Wfg,
           L0_attn_bfg, L0_attn_gamma, L0_attn_Wout, L0_ffn_w_gate, L0_ffn_w_up, L0_ffn_w_down):
    import numpy as np
    import concourse.bacc as bacc
    from concourse.bass_utils import run_bass_kernel_spmd

    def tiles(w):
        a = np.asarray(w).T
        return np.ascontiguousarray(a.reshape(-1, P, a.shape[1]).transpose(1, 0, 2)).reshape(P, -1)

    f32 = np.float32
    w_if = np.zeros((GR, D), f32)
    w_if[0:NH], w_if[32:32 + NH] = L0_attn_Wig, L0_attn_Wfg
    b_if = np.zeros((GR, 1), f32)
    b_if[0:NH, 0], b_if[32:32 + NH, 0] = L0_attn_big, L0_attn_bfg
    w_qk = np.concatenate([np.asarray(L0_attn_Wq), np.asarray(L0_attn_Wk)])
    arrays = {
        "x": np.ascontiguousarray(L0_attn_x).reshape(BATCH * SEQ, D),
        "w_gates": tiles(w_if), "w_qk": tiles(w_qk), "w_v": tiles(L0_attn_Wv), "w_o": tiles(L0_attn_Wog),
        "w_g": tiles(L0_ffn_w_gate), "w_u": tiles(L0_ffn_w_up), "w_d": tiles(L0_ffn_w_down),
        "w_out": tiles(L0_attn_Wout), "gate_bias": b_if,
        "gamma": np.ascontiguousarray(np.asarray(L0_attn_gamma).reshape(KC, P).T),
    }
    nc = bacc.Bacc("TRN2", target_bir_lowering=False, num_devices=1)
    ap = {n: nc.dram_tensor(f"{n}_dram", a.shape, F32, kind="ExternalInput").ap() for n, a in arrays.items()}
    out = nc.dram_tensor("out_dram", (BATCH * SEQ, D), F32, kind="ExternalOutput").ap()
    mlstm_mlp_kernel(nc, ap["x"], {n: ap[f"w_{n}"] for n in WNAMES}, ap["gate_bias"], ap["gamma"], out)
    got = run_bass_kernel_spmd(nc, [{f"{n}_dram": a for n, a in arrays.items()}], core_ids=[0])
    return got.results[0]["out_dram"].reshape(BATCH, SEQ, D)
```

```python
from contextlib import ExitStack

import concourse.bass as bass
from concourse import mybir

ALU = mybir.AluOpType
ACT = mybir.ActivationFunctionType
AX = mybir.AxisListType
F32 = mybir.dt.float32
F32R = mybir.dt.float32r
F16 = mybir.dt.float16
BF16 = mybir.dt.bfloat16
I32 = mybir.dt.int32
R_MAX = bass.bass_isa.ReduceOp.max

P = 128
D = 512
KC = D // P
BATCH, SEQ = 8, 1024
BLOCK = 256
NCH = BLOCK // P
NB = BATCH * SEQ // BLOCK
PER_SEQ = SEQ // BLOCK
NH, DQ, DV = 8, 32, 64
NG = 2
HG = NH // NG
VW = DV + 2
GW = HG * VW
HID = 2048
NJ = HID // P
GR = 40
NU = 2 * NH * DQ

XS = 2.0 ** 8
WS = 2.0 ** 14
HS = 2.0 ** -50
OS = 2.0 ** 10
QKS = 2.0 ** 5
CAP = 15.0
LN_EPS, EPS = 1e-5, 1e-6

USES = (["gates", "q", "k", "v0", "v1", "ffn0", "ffn1", "ffn2", "ffn3", "wT", "ffn4", "wbc", "kT", "ffn5", "o0",
         "ffn6", "st0", "ffn7", "ffn8", "st1", "ffn9", "ffn10", "st2", "ffn11", "hoT0", "ffn12", "st3", "o1",
         "ffn13", "att0", "ffn14", "ffn15", "xT0", "xT1", "hoT1", "att1"])
NUSE = len(USES)
assert NUSE % 3 == 0
TELLS = [n for n in USES if not n.startswith("xT")]


def bank_no(name):
    return USES.index(name) % 3


def uses_told(b, before=NUSE):
    return sum(n in TELLS for n in USES[b:before:3])


AFTER = {j: [] for j in range(NJ)}
AFTER[2] = ["stats"]
AFTER[3] = ["wT"]
AFTER[4] = ["wbc", "kT", "es0"]
AFTER[5] = ["o0", "mean_var"]
AFTER[6] = ["es1", "pv0"]
AFTER[7] = ["xn"]
AFTER[8] = ["es2", "pv1", "center0"]
AFTER[9] = ["scale0"]
AFTER[10] = ["heads0", "es3", "pv2"]
AFTER[11] = ["hoT0"]
AFTER[12] = ["pv3", "o1", "center1"]
AFTER[13] = ["att0", "scale1"]
AFTER[14] = ["heads1"]
AFTER[15] = ["xT0", "xT1", "hoT1"]

WCOLS = {"gates": KC * GR, "qk": KC * NU, "v": KC * D, "o": KC * D, "g": KC * HID, "u": KC * HID, "out": KC * D,
         "d": NJ * D}
WNAMES = list(WCOLS)
PIECES = {n: 4 if c > 4096 else 1 for n, c in WCOLS.items()}
ROUNDS = [["gates", "qk", "v", "o"], ["g"], ["u"], ["out"], ["d"]]
SMALL_COLS = sum(WCOLS[n] for n in ROUNDS[0])
POOL_LOW = {"g": 2, "u": 2}


def dve_pieces(name):
    return PIECES[name] - POOL_LOW.get(name, 0)


def pieces_before(name, k=0):
    return sum(PIECES[n] for n in WNAMES[:WNAMES.index(name)]) + k


def split_before(name, k=0):
    return sum(dve_pieces(n) for n in WNAMES[:WNAMES.index(name)]) + k


def pool_split_before(name, k=0):
    return pieces_before(name) - split_before(name) + k


NPIECES = sum(PIECES.values())
NS = len(WNAMES)


START = 1
DVE_OWN = 58


class Count:

    def __init__(self, sem, per):
        self.sem, self.per, self.k = sem, per, 0

    def step(self, ins):
        self.k += 1
        ins.then_inc(self.sem, 1)

    def settle(self, eng, i):
        eng.wait_ge(self.sem, i * self.per + self.k)

    def close(self):
        assert self.k == self.per, (self.k, self.per)


def mlstm_mlp_kernel(nc, x, w_dram, gate_bias, gamma, out):
    ctx = ExitStack()
    with ctx:
        def sb(name, shape, dt):
            return ctx.enter_context(nc.sbuf_tensor(name, shape, dt))

        def pb(name):
            return ctx.enter_context(nc.psum_tensor(name, [P, 512], F32))

        def sem(name):
            return ctx.enter_context(nc.semaphore(name))

        wt = {n: sb(f"parts_{n}", [P, 2, c], F16) for n, c in WCOLS.items()}
        w_gates = wt["gates"][:, :, :].rearrange("p h (k f) -> p h k f", k=KC)
        w_qk = wt["qk"][:, :, :].rearrange("p h (k f) -> p h k f", k=KC)
        w_v = wt["v"][:, :, :].rearrange("p h (k f) -> p h k f", k=KC)
        w_o = wt["o"][:, :, :].rearrange("p h (k f) -> p h k f", k=KC)
        w_g = wt["g"][:, :, :].rearrange("p h (k f) -> p h k f", k=KC)
        w_u = wt["u"][:, :, :].rearrange("p h (k f) -> p h k f", k=KC)
        w_d = wt["d"][:, :, :].rearrange("p h (j f) -> p h j f", j=NJ)
        w_out = wt["out"][:, :, :].rearrange("p h (k f) -> p h k f", k=KC)

        ident = sb("ident", [P, P], F32)
        spread = sb("spread", [P, NG, P], F32R)
        diag = sb("diag", [P, NH], F32)
        own_head = sb("own_head", [P, GW], F32)
        restart = sb("restart", [NH, BLOCK], F32)
        keep = sb("keep", [P, NB + 1], F32)
        amax = sb("amax", [P, NPIECES], F32)
        amax_pieces = sb("amax_pieces", [P, NPIECES], F32)
        amax_all = sb("amax_all", [P, NS], F32)
        pow2 = sb("pow2", [P, NS], F32)
        wscale = sb("wscale", [P, NS], F32)
        unscale = sb("unscale", [P, NS + 4], F32)
        bias = sb("bias", [GR, 1], F32)
        gam = sb("gam", [P, KC], F32)
        half_pow = sb("half_pow", [P, NH], F32)
        begun = sb("begun", [1, 12], F32)
        ln_eps = sb("ln_eps", [P, NCH], F32)
        xs = sb("xs", [P, NCH], F32)
        minus_xs = sb("minus_xs", [P, NCH], F32)
        sc = {n: i for i, n in enumerate(WNAMES)}

        xt = sb("xt", [P, KC, 2, BLOCK], F16)
        we_r = sb("we_r", [GR, BLOCK], F32R)
        pair_r = sb("pair_r", [P, NH, P], F32R)
        pair_l = sb("pair_l", [P, BLOCK], F32R)

        sizes = [("qs", 512), ("qi", 512), ("kf", 512), ("kt", 512),
                 ("v", NCH * NH * VW), ("to", 512), ("pm", 1024), ("lf", 256), ("ip", 256), ("bc", 256),
                 ("mm", 256), ("upd", GW), ("num", NH * VW),
                 ("hof", 512), ("hoh", 512), ("kp", 512), ("tt", 512), ("hh", 768), ("res", 1024),
                 ("wtok", NCH * 72), ("xn", 1024), ("qq", 1024), ("kk", 1024), ("state", NG * GW), ("wr", 256), ("tg", 256),
                 ("uhl", 256), ("xin", 1024)]
        at, off = {}, 0
        starts = {}
        for name, n in sizes:
            starts[name] = off
            off += n
        arena = sb("arena", [P, off], F32)
        for name, n in sizes:
            at[name] = arena[:, starts[name]:starts[name] + n]
        assert max(SMALL_COLS, WCOLS["out"] + WCOLS["d"]) <= starts["xn"]
        stage, o = {}, 0
        for name in ROUNDS[0]:
            stage[name] = arena[:, o:o + WCOLS[name]]
            o += WCOLS[name]
        stage["g"] = wt["u"][:, :, :].rearrange("p h n -> p (h n)").bitcast(F32)
        stage["u"] = wt["d"][:, :, :].rearrange("p h n -> p (h n)").bitcast(F32)
        stage["out"] = arena[:, 0:WCOLS["out"]]
        stage["d"] = arena[:, WCOLS["out"]:WCOLS["out"] + WCOLS["d"]]
        xin = at["xin"].rearrange("p (c d) -> p c d", c=NCH)
        xn = at["xn"].rearrange("p (c d) -> p c d", c=NCH)

        qs = at["qs"].rearrange("p (g t) -> p g t", g=NG)
        qi = at["qi"].rearrange("p (g t) -> p g t", g=NG)
        qq = at["qq"].bitcast(F16).rearrange("p (g h t) -> p g h t", g=NG, h=HG)
        kk = at["kk"].bitcast(F16).rearrange("p (g h t) -> p g h t", g=NG, h=HG)
        kf = at["kf"].rearrange("p (g t) -> p g t", g=NG)
        kt = at["kt"].rearrange("p (c f) -> p c f", c=NCH)
        v = at["v"].rearrange("p (c h e) -> p c h e", c=NCH, h=NH)
        to = at["to"]
        pm = at["pm"].rearrange("p (b n) -> p b n", b=2)
        tg, lf, ip, bc, mm, wr = (at[n] for n in ("tg", "lf", "ip", "bc", "mm", "wr"))
        uu, aa = bc, ip
        we = at["tg"]
        uhl = at["uhl"].bitcast(F32R)
        a_hi = at["lf"].bitcast(F32R)
        state = at["state"].rearrange("p (g n) -> p g n", g=NG)
        upd = at["upd"]
        num = at["num"].rearrange("p (h e) -> p h e", h=NH)
        sq = at["hof"].rearrange("p (h e) -> p h e", h=NH)
        hof = at["hof"]
        qp = at["hof"].bitcast(F16).rearrange("p (a g t) -> p a g t", a=2, g=NG)
        kp = at["kp"].bitcast(F16).rearrange("p (a g t) -> p a g t", a=2, g=NG)
        ho = at["hoh"].bitcast(F16).rearrange("p (a k t) -> p a k t", a=2, k=KC)
        tt = at["tt"].rearrange("p (b t) -> p b t", b=2)
        HB = 3
        hh = at["hh"].bitcast(F16).rearrange("p (b a t) -> p b a t", b=HB, a=2)
        res = at["res"].rearrange("p (c d) -> p c d", c=NCH)
        wtok = at["wtok"].rearrange("p (c r) -> p c r", c=NCH)
        small = sb("small", [P, 112], F32)[:, :]
        bn6 = small[:, 0:12].rearrange("p (c s) -> p c s", c=NCH)
        mean_var = small[:, 12:16].rearrange("p (c s) -> p c s", c=NCH)
        shift, rstd = small[:, 16:18], small[:, 18:20]
        hsum, mu, den, rden, vsum, var, rd, fac = (small[:, 24 + 8 * n:32 + 8 * n] for n in range(8))
        m_carry = small[0:NH, 96:97]
        decay = small[:, 100:100 + NG * NCH].rearrange("p (g c) -> p g c", g=NG)

        work = [pb(f"work{n}") for n in range(3)]
        acc = [pb(f"acc{c}") for c in range(NCH)]
        e_bank, s_bank, o_bank = pb("e_bank"), pb("s_bank"), pb("o_bank")

        w_loaded = {n: [sem(f"w_loaded_{n}{k}") for k in range(PIECES[n])] for n in WNAMES}
        small_loaded = sem("small_loaded")
        w_max = sem("w_max")
        w_max_all = sem("w_max_all")
        w_gamma = sem("w_gamma")
        w_scaled = sem("w_scaled")
        w_hi = sem("w_hi")
        w_in_place = sem("w_in_place")
        w_split = sem("w_split")
        w_split_pool = sem("w_split_pool")
        w_unscaled = sem("w_unscaled")
        consts = sem("consts")
        dve_set = sem("dve_set")
        pool_set = sem("pool_set")
        ready_set = sem("ready_set")
        first_xt = sem("first_xt")
        x_loaded = sem("x_loaded")
        out_stored = sem("out_stored")
        res_copied = sem("res_copied")
        res_done = sem("res_done")
        work_full = sem("work_full")
        work_free = [sem(f"work_free{n}") for n in range(3)]
        stats_ready = sem("stats_ready")
        factors_ready = sem("factors_ready")
        xn_ready = sem("xn_ready")
        xt_hi = sem("xt_hi")
        xt_ready = sem("xt_ready")
        log_f_ready = sem("log_f_ready")
        rows_ready = sem("rows_ready")
        we_ready = sem("we_ready")
        parts_ready = sem("parts_ready")
        pair_ready = sem("pair_ready")
        e_full = sem("e_full")
        s_full = sem("s_full")
        exp_done = sem("exp_done")
        p_ready = sem("p_ready")
        qk_hi = sem("qk_hi")
        stacks_ready = sem("stacks_ready")
        masked = sem("masked")
        we_split = sem("we_split")
        qi_ready = sem("qi_ready")
        pv_full = sem("pv_full")
        num_ready = sem("num_ready")
        state_ready = sem("state_ready")
        centered = sem("centered")
        squared = sem("squared")
        var_ready = sem("var_ready")
        rd_ready = sem("rd_ready")
        ho_ready = sem("ho_ready")
        ho_hi = sem("ho_hi")
        tanh_done = sem("tanh_done")
        h_hi = sem("h_hi")
        h_ready = sem("h_ready")
        acc_full = sem("acc_full")
        acc_free = sem("acc_free")
        act_own = sem("act_own")
        dve_own = sem("dve_own")
        pool_own = sem("pool_own")

        def amax_of(name, k):
            return amax[:, pieces_before(name, k):pieces_before(name, k) + 1]

        def piece(name, w, k):
            step = WCOLS[name] // PIECES[name]
            return w[:, k * step:(k + 1) * step]

        def bank(name):
            return work[bank_no(name)]

        def free_of(name):
            return work_free[bank_no(name)]

        def wait_bank(eng, i, name):
            n, b = USES.index(name), bank_no(name)
            eng.wait_ge(work_free[b], START + i * uses_told(b) + uses_told(b, n))
            if n >= 3 and USES[n - 3].startswith("xT"):
                eng.wait_ge(xt_ready, NCH * (i + 1) + int(USES[n - 3][-1]) + 1)

        def wait_full(eng, i, name):
            eng.wait_ge(work_full, i * NUSE + USES.index(name) + 1)

        def wait_drained(eng, i, name):
            b = bank_no(name)
            eng.wait_ge(work_free[b], START + i * uses_told(b) + uses_told(b, USES.index(name)) + 1)

        block = ctx.enter_context(nc.Block())
        x_blocks = x.rearrange("(i c p) d -> i p c d", c=NCH, p=P)
        out_blocks = out.rearrange("(i c p) d -> i p c d", c=NCH, p=P)

        @block.sync
        def _(sp):
            sp.dma_start(bias[:, :], gate_bias).then_inc(small_loaded, 16)
            sp.dma_start(gam[:, :], gamma).then_inc(small_loaded, 16)

            def load(n):
                step = WCOLS[n] // PIECES[n]
                for k in range(PIECES[n]):
                    span = slice(k * step, (k + 1) * step)
                    sp.dma_start(stage[n][:, span], w_dram[n][:, span]).then_inc(w_loaded[n][k], 16)

            for n in ROUNDS[0]:
                load(n)
            sp.dma_start(xin, x_blocks[0, :, :, :]).then_inc(x_loaded, 16)
            for n in ("g", "u"):
                load(n)
            sp.wait_ge(w_split, split_before("g"))
            load("out")
            load("d")
            with sp.Fori(0, NB) as i:
                sp.wait_ge(res_copied, NCH * (i + 1))
                sp.dma_start(xin, x_blocks[bass.ds((i + 1) % NB, 1), :, :, :]).then_inc(x_loaded, 16)
                sp.wait_ge(res_done, START + NCH * (i + 1))
                sp.dma_start(out_blocks[bass.ds(i, 1), :, :, :], res).then_inc(out_stored, 16)
            sp.wait_ge(x_loaded, 16 * (NB + 1))
            sp.wait_ge(out_stored, START + 16 * NB)

        @block.gpsimd
        def _(pool):
            g = nc.gpsimd
            own_k = [0]

            def link(ins):
                own_k[0] += 1
                ins.then_inc(pool_set, 1)
                pool.wait_ge(pool_set, own_k[0])

            def norm_factors(i, own):
                own.step(g.tensor_tensor(rstd, mean_var[:, :, 1], ln_eps[:, :], ALU.add))
                own.settle(pool, i)
                own.step(g.tensor_tensor(rstd, rstd, half_pow[:, 0:NCH], ALU.pow))
                own.settle(pool, i)
                own.step(g.tensor_tensor(shift, rstd, minus_xs[:, :], ALU.mult))
                own.settle(pool, i)
                own.step(g.tensor_tensor(rstd, rstd, xs[:, :], ALU.mult))
                g.tensor_tensor(shift, shift, mean_var[:, :, 0], ALU.mult).then_inc(factors_ready, 1)

            link(g.memset(m_carry, 0.0))
            link(g.memset(ident[:, :], 0.0))
            link(g.affine_select(out=ident[:, :], in_=ident[:, :], compare_op=ALU.not_equal, fill=1.0, base=0,
                                 pattern=[[-1, P]], channel_multiplier=1))
            link(g.memset(spread[:, :, :].bitcast(F32), 0.0))
            spread4 = spread[:, :, :].rearrange("p g (h d) -> p g h d", h=HG)
            for first in (0, 32):
                link(g.affine_select(out=spread4, in_=spread4.bitcast(F32), compare_op=ALU.not_equal, fill=1.0,
                                     base=-first, pattern=[[-HG, NG], [-1, HG], [0, DQ]], channel_multiplier=1))
            link(g.memset(we_r[:, :].bitcast(F32), 0.0))
            link(g.memset(diag[:, :], 0.0))
            for first in (0, 32):
                link(g.affine_select(out=diag[:, :], in_=diag[:, :], compare_op=ALU.not_equal, fill=1.0, base=-first,
                                     pattern=[[-1, NH]], channel_multiplier=1))
            link(g.memset(pair_r[:, :, :].bitcast(F32), 0.0))
            for first in (64, 96):
                link(g.affine_select(out=pair_r[:, :, :], in_=pair_r[:, :, :].bitcast(F32),
                                     compare_op=ALU.not_equal, fill=1.0, base=-first,
                                     pattern=[[-1, NH], [0, P]], channel_multiplier=1))
            link(g.memset(pair_l[:, :].bitcast(F32), 0.0))
            link(g.memset(pair_l[0:NH, :].bitcast(F32), -1.0))
            link(g.memset(pair_l[32:32 + NH, :].bitcast(F32), -1.0))
            link(g.memset(own_head[:, :], 0.0))
            for h in range(HG):
                link(g.memset(own_head[h * DQ:(h + 1) * DQ, h * VW:(h + 1) * VW], 1.0))
            link(g.memset(restart[:, :], 1.0))
            link(g.memset(restart[:, 0:BLOCK:P], 0.0))
            link(g.memset(keep[:, :], 1.0))
            link(g.memset(keep[:, 0:NB + 1:PER_SEQ], 0.0))
            link(g.memset(ln_eps[:, :], LN_EPS))
            link(g.memset(xs[:, :], XS))
            link(g.memset(minus_xs[:, :], -XS))
            g.memset(half_pow[:, :], -0.5).then_inc(consts, 1)
            def pool_low_parts(r):
                name = ROUNDS[r][0]
                if name == "u":
                    pool.wait_ge(w_split, split_before(name))
                    pool.wait_ge(w_split_pool, pool_split_before(name))
                for k in range(dve_pieces(name), PIECES[name]):
                    pool.wait_ge(w_hi, pieces_before(name, k) + 1)
                    g.tensor_tensor(piece(name, wt[name][:, 1, :], k), piece(name, stage[name], k),
                                    piece(name, wt[name][:, 0, :], k), ALU.subtract).then_inc(w_split_pool, 1)

            for n, started in enumerate((*work_free, out_stored, res_done, exp_done, p_ready, num_ready, ho_ready,
                                         state_ready)):
                g.memset(begun[0:1, n:n + 1], 0.0).then_inc(started, START)
            for name in ("qq", "kk", "wr", "tg", "state"):
                link(g.memset(at[name], 0.0))
            link(g.memset(uhl.bitcast(F32), 0.0))
            for r, names in enumerate(ROUNDS):
                a, b = pieces_before(names[0]), pieces_before(names[-1], PIECES[names[-1]])
                pool.wait_ge(w_max, r + 1)
                g.partition_all_reduce(amax_pieces[:, a:b], amax[:, a:b], P, R_MAX).then_inc(w_max_all, 1)
                if r == 0:
                    pool.wait_ge(stats_ready, NCH)
                    first = Count(pool_set, 0)
                    first.k = own_k[0]
                    norm_factors(0, first)
                    own_k[0] = first.k
                if r >= 2:
                    pool_low_parts(r - 1)
            pool.wait_ge(w_split, split_before("d", dve_pieces("d")))
            link(g.memset(v[:, :, :, DV:DV + 1], 1.0))
            g.memset(v[:, :, :, DV + 1:VW], 0.0).then_inc(ready_set, 1)
            pool.wait_ge(ready_set, 1)

            with pool.Fori(0, NB) as i:
                own = Count(pool_own, 8)
                def pair(c):
                    g.tensor_tensor(pair_r[0:GR, :, :],
                                    uhl[0:GR, c * P:(c + 1) * P].bitcast(F32).unsqueeze(1).broadcast_to((GR, NH, P)),
                                    diag[0:GR, :].unsqueeze(2).broadcast_to((GR, NH, P)),
                                    ALU.mult).then_inc(pair_ready, 1)

                pool.wait_ge(parts_ready, i + 1)
                pair(0)
                for j in range(NJ):
                    pool.wait_ge(h_hi, i * NJ + j + 1)
                    g.tensor_tensor(hh[:, j % HB, 1, :], tt[:, j % 2, :], hh[:, j % HB, 0, :],
                                    ALU.subtract).then_inc(h_ready, 1)
                    for step in AFTER[j]:
                        if step.startswith("es"):
                            k = int(step[-1])
                            pool.wait_ge(exp_done, START + i * 4 + k + 1)
                            own.step(g.tensor_tensor(begun[0:1, 10:11], half_pow[0:1, 0:1], half_pow[0:1, 1:2],
                                                     ALU.add))
                            rows = pm[:, k % 2, :].rearrange("p (h t) -> p h t", h=HG)
                            g.affine_select(out=rows, in_=rows, compare_op=ALU.is_ge, fill=0.0, base=0,
                                            pattern=[[0, HG], [1, P]], channel_multiplier=-1).then_inc(masked, 1)
                        if step == "es1":
                            pool.wait_ge(e_full, i * 4 + 2)
                            pair(1)
                        if step.startswith("scale"):
                            pool.wait_ge(var_ready, i * NCH + int(step[-1]) + 1)
                            g.tensor_tensor(rd, var, half_pow[:, :], ALU.pow).then_inc(rd_ready, 1)
                        if step == "mean_var":
                            pool.wait_ge(stats_ready, NCH * (i + 2))
                            norm_factors(i, own)
                own.close()

        @block.scalar
        def _(act):
            s = nc.scalar
            def high_parts(r):
                act.wait_ge(w_scaled, r + 1)
                for name in ROUNDS[r]:
                    scale = wscale[:, sc[name]:sc[name] + 1]
                    if name in ("u", "d"):
                        before = {"u": "g", "d": "u"}[name]
                        act.wait_ge(w_split, split_before(before, min(dve_pieces(before), PIECES[name] // 2)))
                    for k in range(PIECES[name]):
                        w = piece(name, stage[name], k)
                        if k >= dve_pieces(name):
                            s.activation(w, w, ACT.Copy, scale=scale).then_inc(w_in_place, 1)
                            act.wait_ge(w_in_place, pool_split_before(name, k - dve_pieces(name)) + 1)
                            s.activation(piece(name, wt[name][:, 0, :], k), w, ACT.Copy).then_inc(w_hi, 1)
                        else:
                            s.activation(piece(name, wt[name][:, 0, :], k), w, ACT.Copy, scale=scale).then_inc(w_hi, 1)

            def out_gamma():
                act.wait_ge(small_loaded, 32)
                act.wait_ge(w_loaded["out"][0], 16)
                for c in range(KC):
                    w = stage["out"][:, c * D:(c + 1) * D]
                    s.activation(w, w, ACT.Copy, scale=gam[:, c:c + 1]).then_inc(w_gamma, 1)

            def x_high(i, c, src):
                s.activation(xt[:, :, 0, c * P:(c + 1) * P], src.rearrange("p (k t) -> p k t", k=KC),
                             ACT.Copy).then_inc(xt_hi, 1)

            def norm_x(i):
                act.wait_ge(factors_ready, i + 1)
                for c in range(NCH):
                    s.activation(xn[:, c, :], xin[:, c, :], ACT.Identity, bias=shift[:, c:c + 1],
                                 scale=rstd[:, c:c + 1]).then_inc(xn_ready, 1)

            high_parts(0)
            norm_x(0)
            for c in range(NCH):
                act.wait_ge(first_xt, c + 1)
                x_high(0, c, (e_bank, s_bank)[c][:, :])
            high_parts(1)
            out_gamma()
            for r in range(2, len(ROUNDS)):
                high_parts(r)
            act.wait_ge(w_unscaled, 1)
            act.wait_ge(ready_set, 1)

            with act.Fori(0, NB) as i:
                own = Count(act_own, 1)
                wait_full(act, i, "gates")
                s.activation(tg[0:GR, :], bank("gates")[0:GR, 0:BLOCK], ACT.Tanh, bias=bias[:, 0:1],
                             scale=unscale[0:GR, 0:1]).then_inc(free_of("gates"), 1)
                wait_drained(act, i, "gates")
                own.step(s.activation(lf[0:NH, :], tg[32:32 + NH, :], ACT.Exp, scale=-CAP))
                own.settle(act, i)
                s.activation(lf[0:NH, :], lf[0:NH, :], ACT.Ln, bias=1.0).then_inc(log_f_ready, 1)
                wait_full(act, i, "q")
                s.activation(at["qs"], bank("q")[:, :], ACT.Copy,
                             scale=unscale[:, NS:NS + 1]).then_inc(free_of("q"), 1)
                wait_full(act, i, "k")
                s.activation(at["kf"], bank("k")[:, :], ACT.Copy,
                             scale=unscale[:, sc["qk"]:sc["qk"] + 1]).then_inc(free_of("k"), 1)
                wait_drained(act, i, "k")
                s.activation(qp[:, 0, :, :], qs, ACT.Copy, scale=unscale[:, NS + 2:NS + 3]).then_inc(qk_hi, 1)
                s.activation(kp[:, 0, :, :], kf, ACT.Copy, scale=unscale[:, NS + 2:NS + 3]).then_inc(qk_hi, 1)
                for c in range(NCH):
                    wait_full(act, i, f"v{c}")
                    s.activation(v[:, c, :, 0:DV], bank(f"v{c}")[:, :].rearrange("p (h e) -> p h e", h=NH), ACT.Copy,
                                 scale=unscale[:, sc["v"]:sc["v"] + 1]).then_inc(free_of(f"v{c}"), 1)
                act.wait_ge(out_stored, START + 16 * i)
                act.wait_ge(x_loaded, 16 * (i + 1))
                for c in range(NCH):
                    s.activation(res[:, c, :], xin[:, c, :], ACT.Copy).then_inc(res_copied, 1)
                for j in range(NJ):
                    wait_full(act, i, f"ffn{j}")
                    if j >= 2:
                        act.wait_ge(h_ready, i * NJ + j - 1)
                    s.activation(tt[:, j % 2, :], bank(f"ffn{j}")[:, 0:BLOCK], ACT.Tanh,
                                 scale=unscale[:, sc["g"]:sc["g"] + 1]).then_inc(tanh_done, 1)
                    wait_drained(act, i, f"ffn{j}")
                    s.activation(hh[:, j % HB, 0, :], tt[:, j % 2, :], ACT.Copy).then_inc(h_hi, 1)
                    if j == 2:
                        act.wait_ge(rows_ready, i + 1)
                        s.activation(we[0:72, :], wr[0:72, :], ACT.Exp).then_inc(we_ready, 1)
                    for step in AFTER[j]:
                        k = int(step[-1]) if step[-1].isdigit() else 0
                        if step == "wT":
                            wait_full(act, i, "wT")
                            s.activation(at["wtok"], bank("wT")[:, 0:NCH * 72], ACT.Copy).then_inc(free_of("wT"), 1)
                        elif step.startswith("es"):
                            act.wait_ge(e_full, i * 4 + k + 1)
                            if k >= 2:
                                act.wait_ge(pv_full, i * 4 + k - 1)
                            s.activation(pm[:, k % 2, :], e_bank[:, :], ACT.Exp).then_inc(exp_done, 1)
                        elif step in ("o0", "o1"):
                            wait_full(act, i, step)
                            act.wait_ge(ho_ready, START + i * NCH + k)
                            s.activation(to, bank(step)[:, :], ACT.Tanh,
                                         scale=unscale[:, sc["o"]:sc["o"] + 1]).then_inc(free_of(step), 1)
                        elif step.startswith("pv"):
                            act.wait_ge(pv_full, i * 4 + k + 1)
                            act.wait_ge(ho_ready, START + i * NCH + k // 2)
                            s.activation(num[:, HG * (k % 2):HG * (k % 2) + HG, :],
                                         o_bank[:, 0:GW].rearrange("p (h e) -> p h e", h=HG),
                                         ACT.Copy).then_inc(num_ready, 1)
                        elif step.startswith("center"):
                            act.wait_ge(centered, i * NCH + k + 1)
                            s.activation(sq, num[:, :, 0:DV], ACT.Square).then_inc(squared, 1)
                        elif step.startswith("hoT"):
                            wait_full(act, i, step)
                            s.activation(ho[:, 0, :, :], bank(step)[:, :].rearrange("p (k t) -> p k t", k=KC),
                                         ACT.Copy).then_inc(ho_hi, 1)
                        elif step == "xn":
                            act.wait_ge(xt_ready, NCH * (i + 1))
                            norm_x(i + 1)
                        elif step.startswith("xT"):
                            wait_full(act, i, step)
                            x_high(i, k, bank(step)[:, :])
                own.close()

        @block.vector
        def _(dve):
            d = nc.vector
            k = [0]

            def link(ins):
                k[0] += 1
                ins.then_inc(dve_set, 1)
                dve.wait_ge(dve_set, k[0])

            def maxima(r):
                if ROUNDS[r] == ["out"]:
                    dve.wait_ge(w_gamma, KC)
                for name in ROUNDS[r]:
                    for k in range(PIECES[name]):
                        dve.wait_ge(w_loaded[name][k], 16)
                        ins = d.tensor_reduce(amax_of(name, k), piece(name, stage[name], k), AX.X, ALU.max,
                                              apply_absolute_value=True)
                        if name == ROUNDS[r][-1] and k == PIECES[name] - 1:
                            ins.then_inc(w_max, 1)
                        else:
                            link(ins)

            def scales(r):
                a, b = sc[ROUNDS[r][0]], sc[ROUNDS[r][-1]] + 1
                dve.wait_ge(w_max_all, r + 1)
                n = pieces_before(ROUNDS[r][0])
                if PIECES[ROUNDS[r][0]] > 1:
                    link(d.tensor_reduce(amax_all[:, a:b], amax_pieces[:, n:n + PIECES[ROUNDS[r][0]]], AX.X,
                                         ALU.max))
                    link(d.tensor_scalar(amax_all[:, a:b], amax_all[:, a:b], 1e-30, None, ALU.max))
                else:
                    link(d.tensor_scalar(amax_all[:, a:b], amax_pieces[:, n:n + b - a], 1e-30, None, ALU.max))
                link(d.tensor_scalar(pow2[:, a:b].bitcast(I32), amax_all[:, a:b].bitcast(I32), 0x7F800000, None,
                                     ALU.bitwise_and))
                link(d.reciprocal(wscale[:, a:b], pow2[:, a:b]))
                d.tensor_scalar(wscale[:, a:b], wscale[:, a:b], WS, None, ALU.mult).then_inc(w_scaled, 1)
                dve.wait_ge(w_scaled, r + 1)

            def low_parts(r):
                for name in ROUNDS[r]:
                    if name in ("u", "d"):
                        dve.wait_ge(w_split, split_before(name))
                        dve.wait_ge(w_split_pool, pool_split_before(name))
                    for k in range(dve_pieces(name)):
                        dve.wait_ge(w_hi, pieces_before(name, k) + 1)
                        d.scalar_tensor_tensor(out=piece(name, wt[name][:, 1, :], k), in0=piece(name, stage[name], k),
                                               scalar=wscale[:, sc[name]:sc[name] + 1],
                                               in1=piece(name, wt[name][:, 0, :], k),
                                               op0=ALU.mult, op1=ALU.subtract).then_inc(w_split, 1)

            def stats(step):
                for c in range(NCH):
                    step(d.bn_stats(bn6[:, c, :], xin[:, c, :]))

            def means():
                for c in range(NCH):
                    d.bn_aggr(mean_var[:, c, :], bn6[:, c, :]).then_inc(stats_ready, 1)

            def x_low(i, c, src):
                dve.wait_ge(xt_hi, NCH * i + c + 1)
                d.tensor_tensor(xt[:, :, 1, c * P:(c + 1) * P], src.rearrange("p (k t) -> p k t", k=KC),
                                xt[:, :, 0, c * P:(c + 1) * P], ALU.subtract).then_inc(xt_ready, 1)

            maxima(0)
            scales(0)
            dve.wait_ge(x_loaded, 16)
            stats(link)
            means()
            low_parts(0)
            maxima(1)
            scales(1)
            maxima(2)
            for c in range(NCH):
                x_low(0, c, (e_bank, s_bank)[c][:, :])
            low_parts(1)
            scales(2)
            maxima(3)
            maxima(4)
            low_parts(2)
            scales(3)
            scales(4)

            back = 1.0 / (XS * WS)
            for name, f in (("gates", back / CAP), ("qk", back), ("v", back), ("o", back / 2), ("g", back / 2),
                            ("out", 1.0 / (WS * OS * 2))):
                link(d.tensor_scalar(unscale[:, sc[name]:sc[name] + 1], pow2[:, sc[name]:sc[name] + 1], f, None,
                                     ALU.mult))
            link(d.tensor_scalar(unscale[:, NS:NS + 1], unscale[:, sc["qk"]:sc["qk"] + 1], float(DQ) ** -0.5, None,
                                 ALU.mult))
            link(d.tensor_tensor(unscale[:, NS + 1:NS + 2], pow2[:, sc["g"]:sc["g"] + 1],
                                 pow2[:, sc["u"]:sc["u"] + 1], ALU.mult))
            link(d.tensor_tensor(unscale[:, NS + 1:NS + 2], unscale[:, NS + 1:NS + 2],
                                 pow2[:, sc["d"]:sc["d"] + 1], ALU.mult))
            link(d.tensor_scalar(unscale[:, NS + 1:NS + 2], unscale[:, NS + 1:NS + 2], 2.0 ** 5 / WS, None, ALU.mult))
            link(d.tensor_scalar(unscale[:, NS + 2:NS + 3], wscale[:, sc["qk"]:sc["qk"] + 1], QKS / WS, None,
                                 ALU.mult))
            link(d.tensor_scalar(unscale[:, NS + 3:NS + 4], pow2[:, sc["qk"]:sc["qk"] + 1], 1.0 / QKS, None,
                                 ALU.mult))
            link(d.tensor_tensor(unscale[:, NS + 3:NS + 4], unscale[:, NS + 3:NS + 4], unscale[:, NS + 3:NS + 4],
                                 ALU.mult))
            dve.wait_ge(small_loaded, 32)
            d.tensor_scalar(bias[:, :], bias[:, :], 1.0 / CAP, None, ALU.mult).then_inc(w_unscaled, 1)

            low_parts(3)
            low_parts(4)

            def add_mlstm(i, c):
                wait_full(dve, i, f"att{c}")
                dve.wait_ge(res_copied, i * NCH + c + 1)
                d.scalar_tensor_tensor(out=res[:, c, :], in0=bank(f"att{c}")[:, :],
                                       scalar=unscale[:, sc["out"]:sc["out"] + 1], in1=res[:, c, :],
                                       op0=ALU.mult, op1=ALU.add).then_inc(free_of(f"att{c}"), 1)

            with dve.Fori(0, NB) as i:
                own = Count(dve_own, DVE_OWN)

                dve.wait_ge(log_f_ready, i + 1)
                own.step(d.tensor_scalar(lf[0:NH, :], lf[0:NH, :], -1.0, None, ALU.mult))
                own.step(d.tensor_scalar(ip[0:NH, :], tg[0:NH, :], CAP, None, ALU.mult))
                own.settle(dve, i)
                own.step(d.tensor_tensor_scan(bc[0:NH, :], restart[:, :], lf[0:NH, :], 0.0, ALU.mult, ALU.add))
                own.step(d.tensor_tensor_scan(mm[0:NH, :], lf[0:NH, :], ip[0:NH, :], m_carry, ALU.add, ALU.max))
                own.settle(dve, i)
                own.step(d.tensor_tensor(aa[0:NH, :], ip[0:NH, :], bc[0:NH, :], ALU.subtract))
                own.settle(dve, i)
                own.step(d.tensor_tensor(uu[0:NH, :], mm[0:NH, :], bc[0:NH, :], ALU.subtract))
                own.settle(dve, i)
                for c in range(NCH):
                    span, end = slice(c * P, (c + 1) * P), c * P + P - 1
                    prev = m_carry if c == 0 else mm[0:NH, c * P - 1:c * P]
                    own.step(d.tensor_scalar(wr[0:NH, span], uu[0:NH, span], prev, -1.0, ALU.subtract, ALU.mult))
                    own.step(d.tensor_scalar(wr[32:32 + NH, span], aa[0:NH, span], uu[0:NH, end:end + 1], None,
                                             ALU.subtract))
                d.tensor_scalar(wr[64:64 + NH, :], mm[0:NH, :], -1.0, None, ALU.mult).then_inc(rows_ready, 1)
                own.step(d.tensor_copy(uhl[0:NH, :], uu[0:NH, :]))
                own.step(d.tensor_copy(a_hi[0:NH, :], aa[0:NH, :]))
                own.step(d.tensor_copy(pair_l[64:64 + NH, :], aa[0:NH, :]))
                own.settle(dve, i)
                own.step(d.tensor_scalar(m_carry, mm[0:NH, BLOCK - 1:BLOCK], keep[0:NH, bass.ds(i + 1, 1)], None,
                                         ALU.mult))
                own.step(d.tensor_tensor(uhl[32:32 + NH, :], uu[0:NH, :], uhl[0:NH, :].bitcast(F32), ALU.subtract))
                d.tensor_tensor(pair_l[96:96 + NH, :], aa[0:NH, :], a_hi[0:NH, :].bitcast(F32),
                                ALU.subtract).then_inc(parts_ready, 1)
                dve.wait_ge(qk_hi, 2 * (i + 1))
                own.step(d.scalar_tensor_tensor(out=qp[:, 1, :, :], in0=qs, scalar=unscale[:, NS + 2:NS + 3],
                                                in1=qp[:, 0, :, :], op0=ALU.mult, op1=ALU.subtract))
                own.step(d.scalar_tensor_tensor(out=kp[:, 1, :, :], in0=kf, scalar=unscale[:, NS + 2:NS + 3],
                                                in1=kp[:, 0, :, :], op0=ALU.mult, op1=ALU.subtract))
                own.settle(dve, i)
                for h in range(HG):
                    rows = slice(h * DQ, (h + 1) * DQ)
                    for n, (q_part, k_part) in enumerate(((0, 0), (1, 0), (0, 1))):
                        to_ = slice((h + n) % HG * DQ, ((h + n) % HG + 1) * DQ)
                        d.tensor_copy(qq[to_, :, h, :], qp[rows, q_part, :, :]).then_inc(stacks_ready, 1)
                        d.tensor_copy(kk[to_, :, h, :], kp[rows, k_part, :, :]).then_inc(stacks_ready, 1)

                for j in range(NJ):
                    b = bank(f"ffn{j}")
                    dve.wait_ge(tanh_done, i * NJ + j + 1)
                    own.step(d.scalar_tensor_tensor(out=tt[:, j % 2, :], in0=tt[:, j % 2, :], scalar=1.0,
                                                    in1=b[:, 0:BLOCK], op0=ALU.add, op1=ALU.mult))
                    own.settle(dve, i)
                    d.scalar_tensor_tensor(out=tt[:, j % 2, :], in0=tt[:, j % 2, :], scalar=HS,
                                           in1=b[:, BLOCK:2 * BLOCK], op0=ALU.mult,
                                           op1=ALU.mult).then_inc(free_of(f"ffn{j}"), 1)
                    for step in AFTER[j]:
                        k_ = int(step[-1]) if step[-1].isdigit() else 0
                        if step == "stats":
                            dve.wait_ge(x_loaded, 16 * (i + 2))
                            stats(own.step)
                        elif step == "wT":
                            dve.wait_ge(we_ready, i + 1)
                            own.step(d.tensor_copy(we_r[0:NH, :], we[0:NH, :]))
                            own.settle(dve, i)
                            d.tensor_tensor(we_r[32:32 + NH, :], we[0:NH, :], we_r[0:NH, :].bitcast(F32),
                                            ALU.subtract).then_inc(we_split, 1)
                        elif step == "mean_var":
                            means()
                        elif step == "wbc":
                            wb = bank("wbc")[:, :].rearrange("p (g t) -> p g t", g=NG)
                            wait_full(dve, i, "wbc")
                            wait_drained(dve, i, "q")
                            d.tensor_tensor(at["qi"], at["qs"], bank("wbc")[:, :], ALU.mult).then_inc(qi_ready, 1)
                            d.tensor_copy(decay, wb[:, :, P - 1:BLOCK:P]).then_inc(free_of("wbc"), 1)
                        elif step == "kT":
                            wait_full(dve, i, "kT")
                            wait_drained(dve, i, "wT")
                            d.tensor_tensor(kt[:, :, :].rearrange("p c (h e) -> p c h e", h=NH),
                                            bank("kT")[:, :].rearrange("p (c h e) -> p c h e", c=NCH, h=NH),
                                            wtok[:, :, 32:32 + NH].unsqueeze(3).broadcast_to((P, NCH, NH, DQ)),
                                            ALU.mult).then_inc(free_of("kT"), 1)
                        elif step.startswith("es"):
                            dve.wait_ge(s_full, i * 4 + k_ + 1)
                            dve.wait_ge(masked, i * 4 + k_ + 1)
                            d.scalar_tensor_tensor(out=pm[:, k_ % 2, :], in0=s_bank[:, :],
                                                   scalar=unscale[:, NS + 3:NS + 4], in1=pm[:, k_ % 2, :],
                                                   op0=ALU.mult, op1=ALU.mult).then_inc(p_ready, 1)
                        elif step.startswith("pv"):
                            c, g = k_ // 2, k_ % 2
                            wait_full(dve, i, f"st{k_}")
                            wait_drained(dve, i, "wbc")
                            d.tensor_tensor(upd, own_head[:, :], bank(f"st{k_}")[:, 0:GW],
                                            ALU.mult).then_inc(free_of(f"st{k_}"), 1)
                            wait_drained(dve, i, f"st{k_}")
                            d.scalar_tensor_tensor(out=state[:, g, :], in0=state[:, g, :],
                                                   scalar=decay[:, g, c:c + 1], in1=upd, op0=ALU.mult,
                                                   op1=ALU.add).then_inc(state_ready, 1)
                            if k_ == 3:
                                dve.wait_ge(state_ready, START + i * 5 + 4)
                                d.tensor_scalar(at["state"], at["state"], keep[:, bass.ds(i + 1, 1)], None,
                                                ALU.mult).then_inc(state_ready, 1)
                        elif step.startswith("center"):
                            dve.wait_ge(num_ready, START + i * 4 + 2 * k_ + 2)
                            own.step(d.tensor_reduce(hsum, num[:, :, 0:DV], AX.X, ALU.add))
                            own.settle(dve, i)
                            own.step(d.tensor_scalar(mu, hsum, 1.0 / DV, None, ALU.mult))
                            own.settle(dve, i)
                            d.tensor_tensor(num[:, :, 0:DV], num[:, :, 0:DV],
                                            mu.unsqueeze(2).broadcast_to((P, NH, DV)),
                                            ALU.subtract).then_inc(centered, 1)
                            own.step(d.scalar_tensor_tensor(out=den, in0=num[:, :, DV], scalar=-1.0,
                                                            in1=wtok[:, k_, 64:64 + NH], op0=ALU.mult, op1=ALU.max))
                            own.settle(dve, i)
                            own.step(d.tensor_tensor(den, den, num[:, :, DV], ALU.max))
                            own.settle(dve, i)
                            own.step(d.tensor_scalar(den, den, EPS, None, ALU.add))
                            own.settle(dve, i)
                            own.step(d.reciprocal(rden, den))
                        elif step.startswith("scale"):
                            dve.wait_ge(squared, i * NCH + k_ + 1)
                            own.step(d.tensor_reduce(vsum, sq, AX.X, ALU.add))
                            own.settle(dve, i)
                            own.step(d.tensor_tensor(vsum, vsum, rden, ALU.mult))
                            own.settle(dve, i)
                            own.step(d.tensor_tensor(vsum, vsum, rden, ALU.mult))
                            own.settle(dve, i)
                            d.tensor_scalar(var, vsum, 1.0 / DV, EPS, ALU.mult, ALU.add).then_inc(var_ready, 1)
                        elif step.startswith("heads"):
                            dve.wait_ge(rd_ready, i * NCH + k_ + 1)
                            own.step(d.scalar_tensor_tensor(out=fac, in0=rden, scalar=OS, in1=rd, op0=ALU.mult,
                                                            op1=ALU.mult))
                            own.settle(dve, i)
                            own.step(d.tensor_tensor(num[:, :, 0:DV], num[:, :, 0:DV],
                                                     fac.unsqueeze(2).broadcast_to((P, NH, DV)), ALU.mult))
                            own.settle(dve, i)
                            wait_drained(dve, i, f"o{k_}")
                            d.scalar_tensor_tensor(out=hof.rearrange("p (h e) -> p h e", h=NH),
                                                   in0=to.rearrange("p (h e) -> p h e", h=NH), scalar=1.0,
                                                   in1=num[:, :, 0:DV], op0=ALU.add,
                                                   op1=ALU.mult).then_inc(ho_ready, 1)
                        elif step.startswith("hoT"):
                            dve.wait_ge(ho_hi, i * NCH + k_ + 1)
                            d.tensor_tensor(ho[:, 1, :, :], bank(step)[:, :].rearrange("p (k t) -> p k t", k=KC),
                                            ho[:, 0, :, :], ALU.subtract).then_inc(free_of(step), 1)
                        elif step.startswith("xT"):
                            x_low(i + 1, k_, bank(step)[:, :])
                        elif step == "att0":
                            add_mlstm(i, 0)
                add_mlstm(i, 1)
                for c in range(NCH):
                    dve.wait_ge(acc_full, i * NCH + c + 1)
                    wait_drained(dve, i, f"att{c}")
                    d.scalar_tensor_tensor(out=res[:, c, :], in0=acc[c][:, :], scalar=unscale[:, NS + 1:NS + 2],
                                           in1=res[:, c, :], op0=ALU.mult, op1=ALU.add).then_inc(res_done, 1)
                own.close()

        @block.tensor
        def _(pe):
            t = nc.tensor

            def three(dst, w, a, first, last):
                t.matmul(dst, w[0], a[0], start=first, stop=False, skip_group_check=True)
                t.matmul(dst, w[0], a[1], start=False, stop=False, skip_group_check=True)
                return t.matmul(dst, w[1], a[0], start=False, stop=last, skip_group_check=True)

            def by_feature(dst, w, f0, f1):
                for k in range(KC):
                    mm_ = three(dst, (w[:, 0, k, f0:f1], w[:, 1, k, f0:f1]), (xt[:, k, 0, :], xt[:, k, 1, :]),
                                k == 0, k == KC - 1)
                return mm_

            def by_token(dst, c, w):
                span = slice(c * P, (c + 1) * P)
                for k in range(KC):
                    mm_ = three(dst, (xt[:, k, 0, span], xt[:, k, 1, span]), (w[:, 0, k, :], w[:, 1, k, :]),
                                k == 0, k == KC - 1)
                return mm_

            pe.wait_ge(consts, 1)
            for c in range(NCH):
                pe.wait_ge(xn_ready, c + 1)
                for k in range(KC):
                    tr = t.transpose((e_bank, s_bank)[c][:, k * P:(k + 1) * P], xn[:, c, k * P:(k + 1) * P],
                                     ident[:, :])
                tr.then_inc(first_xt, 1)

            with pe.Fori(0, NB) as i:
                def down(j):
                    pe.wait_ge(h_ready, i * NJ + j + 1)
                    for c in range(NCH):
                        if j == 0:
                            pe.wait_ge(res_done, START + i * NCH)
                        span = slice(c * P, (c + 1) * P)
                        h = hh[:, j % HB, :, :]
                        mm_ = three(acc[c][:, :], (h[:, 0, span], h[:, 1, span]), (w_d[:, 0, j, :], w_d[:, 1, j, :]),
                                    j == 0, j == NJ - 1)
                        if j == NJ - 1:
                            mm_.then_inc(acc_full, 1)

                def project(c):
                    wait_drained(pe, i, f"hoT{c}")
                    for n in range(KC):
                        mm_ = three(bank(f"att{c}")[:, :], (ho[:, 0, n, :], ho[:, 1, n, :]),
                                    (w_out[:, 0, n, :], w_out[:, 1, n, :]), n == 0, n == KC - 1)
                    mm_.then_inc(work_full, 1)

                pe.wait_ge(xt_ready, NCH * (i + 1))
                wait_bank(pe, i, "gates")
                by_feature(bank("gates")[0:GR, 0:BLOCK], w_gates, 0, GR).then_inc(work_full, 1)
                for name, f in (("q", 0), ("k", NH * DQ)):
                    wait_bank(pe, i, name)
                    for g in range(NG):
                        mm_ = by_feature(bank(name)[:, g * BLOCK:(g + 1) * BLOCK], w_qk, f + g * P, f + (g + 1) * P)
                    mm_.then_inc(work_full, 1)
                for c in range(NCH):
                    wait_bank(pe, i, f"v{c}")
                    by_token(bank(f"v{c}")[:, :], c, w_v).then_inc(work_full, 1)

                for j in range(NJ):
                    name = f"ffn{j}"
                    wait_bank(pe, i, name)
                    by_feature(bank(name)[:, 0:BLOCK], w_g, j * P, (j + 1) * P)
                    by_feature(bank(name)[:, BLOCK:2 * BLOCK], w_u, j * P, (j + 1) * P).then_inc(work_full, 1)
                    if j >= 2:
                        down(j - 2)
                    for step in AFTER[j]:
                        k = int(step[-1]) if step[-1].isdigit() else 0
                        if step in USES:
                            wait_bank(pe, i, step)
                        if step == "wT":
                            pe.wait_ge(we_ready, i + 1)
                            for c in range(NCH):
                                tr = t.transpose(bank(step)[:, c * 72:(c + 1) * 72], we[0:72, c * P:(c + 1) * P],
                                                 ident[0:72, 0:72])
                            tr.then_inc(work_full, 1)
                        elif step == "wbc":
                            pe.wait_ge(we_split, i + 1)
                            for g in range(NG):
                                mm_ = t.matmul(bank(step)[:, g * BLOCK:(g + 1) * BLOCK], spread[0:GR, g, :],
                                               we_r[:, :], start=True, stop=True)
                            mm_.then_inc(work_full, 1)
                        elif step == "kT":
                            wait_drained(pe, i, "k")
                            for c in range(NCH):
                                for g in range(NG):
                                    n = c * NG + g
                                    tr = t.transpose(bank(step)[:, n * P:(n + 1) * P], kf[:, g, c * P:(c + 1) * P],
                                                     ident[:, :])
                            tr.then_inc(work_full, 1)
                        elif step.startswith("es"):
                            c, g = k // 2, k % 2
                            span = slice(c * P, (c + 1) * P)
                            pe.wait_ge(pair_ready, i * NCH + c + 1)
                            pe.wait_ge(exp_done, START + i * 4 + k)
                            t.matmul(e_bank[:, :], pair_l[:, span], pair_r[:, g * HG:(g + 1) * HG, :], start=True,
                                     stop=True).then_inc(e_full, 1)
                            pe.wait_ge(stacks_ready, (i + 1) * 6 * HG)
                            pe.wait_ge(p_ready, START + i * 4 + k)
                            for h in range(HG):
                                mm_ = t.matmul(s_bank[:, h * P:(h + 1) * P], kk[:, g, h, span], qq[:, g, h, span],
                                               start=True, stop=True)
                            mm_.then_inc(s_full, 1)
                        elif step in ("o0", "o1"):
                            by_token(bank(step)[:, :], k, w_o).then_inc(work_full, 1)
                        elif step.startswith("pv"):
                            c, g = k // 2, k % 2
                            span = slice(c * P, (c + 1) * P)
                            pe.wait_ge(qi_ready, i + 1)
                            pe.wait_ge(state_ready, START + i * 5 + (k - 1 if c else 0))
                            pe.wait_ge(num_ready, START + i * 4 + k)
                            t.matmul(o_bank[:, 0:GW], qi[:, g, span], state[:, g, :], start=True, stop=False,
                                     skip_group_check=True)
                            wait_drained(pe, i, f"v{c}")
                            pe.wait_ge(p_ready, START + i * 4 + k + 1)
                            for h in range(HG):
                                mm_ = t.matmul(o_bank[:, h * VW:(h + 1) * VW], pm[:, k % 2, h * P:(h + 1) * P],
                                               v[:, c, g * HG + h, :], start=False, stop=(h == HG - 1),
                                               skip_group_check=True)
                            mm_.then_inc(pv_full, 1)
                            wait_bank(pe, i, f"st{k}")
                            wait_drained(pe, i, "kT")
                            t.matmul(bank(f"st{k}")[:, 0:GW], kt[:, c, g * P:(g + 1) * P],
                                     v[:, c, g * HG:(g + 1) * HG, :], start=True,
                                     stop=True).then_inc(work_full, 1)
                        elif step.startswith("hoT"):
                            pe.wait_ge(ho_ready, START + i * NCH + k + 1)
                            for n in range(KC):
                                tr = t.transpose(bank(step)[:, n * P:(n + 1) * P], hof[:, n * P:(n + 1) * P],
                                                 ident[:, :])
                            tr.then_inc(work_full, 1)
                        elif step == "att0":
                            project(0)
                        elif step.startswith("xT"):
                            pe.wait_ge(xn_ready, NCH * (i + 1) + k + 1)
                            for n in range(KC):
                                tr = t.transpose(bank(step)[:, n * P:(n + 1) * P], xn[:, k, n * P:(n + 1) * P],
                                                 ident[:, :])
                            tr.then_inc(work_full, 1)
                down(NJ - 2)
                down(NJ - 1)
                wait_bank(pe, i, "att1")
                project(1)


def kernel(L0_attn_x, L0_attn_Wq, L0_attn_Wk, L0_attn_Wv, L0_attn_Wog, L0_attn_Wig, L0_attn_big, L0_attn_Wfg,
           L0_attn_bfg, L0_attn_gamma, L0_attn_Wout, L0_ffn_w_gate, L0_ffn_w_up, L0_ffn_w_down):
    import numpy as np
    import concourse.bacc as bacc
    from concourse.bass_utils import run_bass_kernel_spmd

    def tiles(w):
        a = np.asarray(w).T
        return np.ascontiguousarray(a.reshape(-1, P, a.shape[1]).transpose(1, 0, 2)).reshape(P, -1)

    f32 = np.float32
    w_if = np.zeros((GR, D), f32)
    w_if[0:NH], w_if[32:32 + NH] = L0_attn_Wig, L0_attn_Wfg
    b_if = np.zeros((GR, 1), f32)
    b_if[0:NH, 0], b_if[32:32 + NH, 0] = L0_attn_big, L0_attn_bfg
    w_qk = np.concatenate([np.asarray(L0_attn_Wq), np.asarray(L0_attn_Wk)])
    arrays = {
        "x": np.ascontiguousarray(L0_attn_x).reshape(BATCH * SEQ, D),
        "w_gates": tiles(w_if), "w_qk": tiles(w_qk), "w_v": tiles(L0_attn_Wv), "w_o": tiles(L0_attn_Wog),
        "w_g": tiles(L0_ffn_w_gate), "w_u": tiles(L0_ffn_w_up), "w_d": tiles(L0_ffn_w_down),
        "w_out": tiles(L0_attn_Wout), "gate_bias": b_if,
        "gamma": np.ascontiguousarray(np.asarray(L0_attn_gamma).reshape(KC, P).T),
    }
    nc = bacc.Bacc("TRN2", target_bir_lowering=False, num_devices=1)
    ap = {n: nc.dram_tensor(f"{n}_dram", a.shape, F32, kind="ExternalInput").ap() for n, a in arrays.items()}
    out = nc.dram_tensor("out_dram", (BATCH * SEQ, D), F32, kind="ExternalOutput").ap()
    mlstm_mlp_kernel(nc, ap["x"], {n: ap[f"w_{n}"] for n in WNAMES}, ap["gate_bias"], ap["gamma"], out)
    got = run_bass_kernel_spmd(nc, [{f"{n}_dram": a for n, a in arrays.items()}], core_ids=[0])
    return got.results[0]["out_dram"].reshape(BATCH, SEQ, D)
```

```python
from contextlib import ExitStack

import concourse.bass as bass
from concourse import mybir

ALU = mybir.AluOpType
ACT = mybir.ActivationFunctionType
AX = mybir.AxisListType
F32 = mybir.dt.float32
F32R = mybir.dt.float32r
F16 = mybir.dt.float16
BF16 = mybir.dt.bfloat16
I32 = mybir.dt.int32
R_MAX = bass.bass_isa.ReduceOp.max

P = 128
D = 512
KC = D // P
BATCH, SEQ = 8, 1024
BLOCK = 256
NCH = BLOCK // P
NB = BATCH * SEQ // BLOCK
PER_SEQ = SEQ // BLOCK
NH, DQ, DV = 8, 32, 64
NG = 2
HG = NH // NG
assert HG == KC
VW = DV + 2
GW = HG * VW
HID = 2048
NJ = HID // P
GR = 40
G_LOW = 64
NU = 2 * NH * DQ

XS = 2.0 ** 8
WS = 2.0 ** 14
HS = 2.0 ** -50
OS = 2.0 ** 10
QKS = 2.0 ** 5
CAP = 15.0
LN_EPS, EPS = 1e-5, 1e-6

USES = (["gates", "q", "k", "v0", "v1", "ffn0", "ffn1", "ffn2", "ffn3", "wT", "ffn4", "wbc", "kT", "ffn5", "o0",
         "ffn6", "st0", "ffn7", "ffn8", "st1", "ffn9", "ffn10", "st2", "ffn11", "ffn12", "st3", "o1",
         "ffn13", "att0", "ffn14", "ffn15", "hoT1", "att1"])
NUSE = len(USES)
assert NUSE % 3 == 0


def bank_no(name):
    return USES.index(name) % 3


def uses_of(b, before=NUSE):
    return len(USES[b:before:3])


AFTER = {j: [] for j in range(NJ)}
AFTER[0] = ["stack3"]
AFTER[2] = ["stats"]
AFTER[3] = ["wT"]
AFTER[4] = ["wbc", "kT", "es0"]
AFTER[5] = ["o0", "mean_var"]
AFTER[6] = ["es1", "pv0", "xn0"]
AFTER[7] = ["turn00", "turn01"]
AFTER[8] = ["es2", "pv1", "center0", "turn02"]
AFTER[9] = ["scale0", "turn03", "xn1"]
AFTER[10] = ["heads0", "es3", "pv2", "hoTurn0", "hoTurn1"]
AFTER[11] = ["hoTurn2", "hoTurn3", "hoT0"]
AFTER[12] = ["pv3", "o1", "center1", "turn10"]
AFTER[13] = ["att0", "scale1", "turn11"]
AFTER[14] = ["heads1", "turn12", "turn13"]
AFTER[15] = ["hoT1", "xT0", "xT1"]

UNIT_IN = {j + 1: int(step[-1]) for j in AFTER for step in AFTER[j] if step.startswith("pv")}

WCOLS = {"gates": KC * GR, "qk": KC * NU, "v": KC * D, "o": KC * D, "g": KC * HID, "u": KC * HID, "out": KC * D,
         "d": NJ * D}
WNAMES = list(WCOLS)
PIECES = {n: 4 if c > 4096 else 1 for n, c in WCOLS.items()}
ROUNDS = [["gates", "qk", "v", "o"], ["g"], ["u"], ["out"], ["d"]]
SMALL_COLS = sum(WCOLS[n] for n in ROUNDS[0])
POOL_LOW = {"v": 1, "o": 1, "g": 3, "u": 2, "out": 1}


def dve_pieces(name):
    return PIECES[name] - POOL_LOW.get(name, 0)


def pieces_before(name, k=0):
    return sum(PIECES[n] for n in WNAMES[:WNAMES.index(name)]) + k


def split_before(name, k=0):
    return sum(dve_pieces(n) for n in WNAMES[:WNAMES.index(name)]) + k


def pool_split_before(name, k=0):
    return pieces_before(name) - split_before(name) + k


NPIECES = sum(PIECES.values())
NS = len(WNAMES)


START = 1
TURNS = 16
DVE_OWN = 58


class Count:

    def __init__(self, sem, per):
        self.sem, self.per, self.k = sem, per, 0

    def step(self, ins):
        self.k += 1
        ins.then_inc(self.sem, 1)

    def settle(self, eng, i):
        eng.wait_ge(self.sem, i * self.per + self.k)

    def close(self):
        assert self.k == self.per, (self.k, self.per)


def mlstm_mlp_kernel(nc, x, w_dram, gate_bias, gamma, out):
    ctx = ExitStack()
    with ctx:
        def sb(name, shape, dt):
            return ctx.enter_context(nc.sbuf_tensor(name, shape, dt))

        def pb(name):
            return ctx.enter_context(nc.psum_tensor(name, [P, 512], F32))

        def sem(name):
            return ctx.enter_context(nc.semaphore(name))

        wt = {n: sb(f"parts_{n}", [P, 2, c], F16) for n, c in WCOLS.items() if n != "gates"}
        w_gates = sb("parts_gates", [P, KC, G_LOW + GR], F16)
        w_qk = wt["qk"][:, :, :].rearrange("p h (k f) -> p h k f", k=KC)
        w_v = wt["v"][:, :, :].rearrange("p h (k f) -> p h k f", k=KC)
        w_o = wt["o"][:, :, :].rearrange("p h (k f) -> p h k f", k=KC)
        w_g = wt["g"][:, :, :].rearrange("p h (k f) -> p h k f", k=KC)
        w_u = wt["u"][:, :, :].rearrange("p h (k f) -> p h k f", k=KC)
        w_d = wt["d"][:, :, :].rearrange("p h (j f) -> p h j f", j=NJ)
        w_out = wt["out"][:, :, :].rearrange("p h (k f) -> p h k f", k=KC)

        ident = sb("ident", [P, P], F32)
        spread = sb("spread", [P, NG, P], F32R)
        diag = sb("diag", [P, NH], F32)
        own_head = sb("own_head", [P, GW], F32)
        restart = sb("restart", [NH, BLOCK], F32)
        keep = sb("keep", [P, NB + 1], F32)
        amax = sb("amax", [P, NPIECES], F32)
        amax_pieces = sb("amax_pieces", [P, NPIECES], F32)
        amax_all = sb("amax_all", [P, NS], F32)
        pow2 = sb("pow2", [P, NS], F32)
        wscale = sb("wscale", [P, NS], F32)
        unscale = sb("unscale", [P, NS + 4], F32)
        bias = sb("bias", [GR, 1], F32)
        gam = sb("gam", [P, KC], F32)
        half_pow = sb("half_pow", [P, NH], F32)
        begun = sb("begun", [1, 16], F32)
        ln_eps = sb("ln_eps", [P, NCH], F32)
        xs = sb("xs", [P, NCH], F32)
        minus_xs = sb("minus_xs", [P, NCH], F32)
        sc = {n: i for i, n in enumerate(WNAMES)}

        xt = sb("xt", [P, KC, 2, BLOCK], F16)
        we_r = sb("we_r", [GR, BLOCK], F32R)
        pair_r = sb("pair_r", [P, NH, P], F32R)
        pair_l = sb("pair_l", [P, BLOCK], F32R)

        sizes = [("qs", 512), ("qi", 512), ("kf", 512), ("kt", 512),
                 ("v", NCH * NH * VW), ("to", 512), ("pm", 1024), ("lf", 256), ("ip", 256), ("bc", 256),
                 ("mm", 256), ("upd", GW), ("num", NH * VW),
                 ("hof", 512), ("hoh", 512), ("kp", 512), ("tt", 512), ("hh", 768), ("res", 1024),
                 ("wtok", NCH * 72), ("xn", D), ("xnt", NCH * KC * P), ("qq", 1024), ("kk", 1024),
                 ("state", NG * GW), ("wr", 256), ("tg", 256), ("uhl", 256), ("xin", 1024)]
        at, off = {}, 0
        starts = {}
        for name, n in sizes:
            starts[name] = off
            off += n
        arena = sb("arena", [P, off], F32)
        for name, n in sizes:
            at[name] = arena[:, starts[name]:starts[name] + n]
        assert max(SMALL_COLS, WCOLS["out"] + WCOLS["d"]) <= starts["xn"]
        stage, o = {}, 0
        for name in ROUNDS[0]:
            stage[name] = arena[:, o:o + WCOLS[name]]
            o += WCOLS[name]
        stage["g"] = wt["u"][:, :, :].rearrange("p h n -> p (h n)").bitcast(F32)
        stage["u"] = wt["d"][:, :, :].rearrange("p h n -> p (h n)").bitcast(F32)
        stage["out"] = arena[:, 0:WCOLS["out"]]
        stage["d"] = arena[:, WCOLS["out"]:WCOLS["out"] + WCOLS["d"]]
        xin = at["xin"].rearrange("p (c d) -> p c d", c=NCH)
        xn = at["xn"]
        xnt = at["xnt"].rearrange("p (c k t) -> p c k t", c=NCH, k=KC)

        qs = at["qs"].rearrange("p (g t) -> p g t", g=NG)
        qi = at["qi"].rearrange("p (g t) -> p g t", g=NG)
        qq = at["qq"].bitcast(F16).rearrange("p (g h t) -> p g h t", g=NG, h=HG)
        kk = at["kk"].bitcast(F16).rearrange("p (g h t) -> p g h t", g=NG, h=HG)
        kf = at["kf"].rearrange("p (g t) -> p g t", g=NG)
        kt = at["kt"].rearrange("p (c f) -> p c f", c=NCH)
        v = at["v"].rearrange("p (c h e) -> p c h e", c=NCH, h=NH)
        to = at["to"]
        pm = at["pm"].rearrange("p (b n) -> p b n", b=2)
        tg, lf, ip, bc, mm, wr = (at[n] for n in ("tg", "lf", "ip", "bc", "mm", "wr"))
        uu, aa = bc, ip
        we = at["tg"]
        uhl = at["uhl"].bitcast(F32R)
        a_hi = at["lf"].bitcast(F32R)
        state = at["state"].rearrange("p (g n) -> p g n", g=NG)
        upd = at["upd"]
        num = at["num"].rearrange("p (h e) -> p h e", h=NH)
        sq = at["hof"].rearrange("p (h e) -> p h e", h=NH)
        hof = at["hof"]
        qp = at["hof"].bitcast(F16).rearrange("p (a g t) -> p a g t", a=2, g=NG)
        kp = at["kp"].bitcast(F16).rearrange("p (a g t) -> p a g t", a=2, g=NG)
        ho = at["hoh"].bitcast(F16).rearrange("p (a k t) -> p a k t", a=2, k=KC)
        tt = at["tt"].rearrange("p (b t) -> p b t", b=2)
        HB = 3
        hh = at["hh"].bitcast(F16).rearrange("p (b a t) -> p b a t", b=HB, a=2)
        res = at["res"].rearrange("p (c d) -> p c d", c=NCH)
        wtok = at["wtok"].rearrange("p (c r) -> p c r", c=NCH)
        small = sb("small", [P, 112], F32)[:, :]
        bn6 = small[:, 0:12].rearrange("p (c s) -> p c s", c=NCH)
        mean_var = small[:, 12:16].rearrange("p (c s) -> p c s", c=NCH)
        shift, rstd = small[:, 16:18], small[:, 18:20]
        hsum, mu, den, rden, vsum, var, rd, fac = (small[:, 24 + 8 * n:32 + 8 * n] for n in range(8))
        m_carry = small[0:NH, 96:97]
        decay = small[:, 100:100 + NG * NCH].rearrange("p (g c) -> p g c", g=NG)

        work = [pb(f"work{n}") for n in range(3)]
        acc = [pb(f"acc{c}") for c in range(NCH)]
        e_bank, s_bank, o_bank = pb("e_bank"), pb("s_bank"), pb("o_bank")

        w_loaded = {n: [sem(f"w_loaded_{n}{k}") for k in range(PIECES[n])] for n in WNAMES}
        small_loaded = sem("small_loaded")
        w_max = sem("w_max")
        w_max_all = sem("w_max_all")
        w_gamma = sem("w_gamma")
        w_scaled = sem("w_scaled")
        w_hi = sem("w_hi")
        w_in_place = sem("w_in_place")
        w_split = sem("w_split")
        w_split_pool = sem("w_split_pool")
        w_unscaled = sem("w_unscaled")
        consts = sem("consts")
        dve_set = sem("dve_set")
        pool_set = sem("pool_set")
        ready_set = sem("ready_set")
        first_xt = sem("first_xt")
        x_loaded = sem("x_loaded")
        out_stored = sem("out_stored")
        res_copied = sem("res_copied")
        res_done = sem("res_done")
        work_full = sem("work_full")
        work_free = [sem(f"work_free{n}") for n in range(3)]
        stats_ready = sem("stats_ready")
        factors_ready = sem("factors_ready")
        xn_ready = sem("xn_ready")
        xn_turned = sem("xn_turned")
        xt_hi = sem("xt_hi")
        ho_turned = sem("ho_turned")
        ho_split = sem("ho_split")
        xt_ready = sem("xt_ready")
        gates_low = sem("gates_low")
        log_f_ready = sem("log_f_ready")
        rows_ready = sem("rows_ready")
        we_ready = sem("we_ready")
        parts_ready = sem("parts_ready")
        pair_ready = sem("pair_ready")
        e_full = sem("e_full")
        s_full = sem("s_full")
        exp_done = sem("exp_done")
        p_ready = sem("p_ready")
        qk_hi = sem("qk_hi")
        stacks_ready = sem("stacks_ready")
        masked = sem("masked")
        we_split = sem("we_split")
        qi_ready = sem("qi_ready")
        pv_full = sem("pv_full")
        num_ready = sem("num_ready")
        state_ready = sem("state_ready")
        centered = sem("centered")
        squared = sem("squared")
        var_ready = sem("var_ready")
        rd_ready = sem("rd_ready")
        ho_ready = sem("ho_ready")
        ho_hi = sem("ho_hi")
        tanh_done = sem("tanh_done")
        h_hi = sem("h_hi")
        h_ready = sem("h_ready")
        acc_full = sem("acc_full")
        acc_free = sem("acc_free")
        act_own = sem("act_own")
        dve_own = sem("dve_own")
        pool_own = sem("pool_own")

        def amax_of(name, k):
            return amax[:, pieces_before(name, k):pieces_before(name, k) + 1]

        def piece(name, w, k):
            step = WCOLS[name] // PIECES[name]
            return w[:, k * step:(k + 1) * step]

        def part(name, n, k):
            if name == "gates":
                return w_gates[:, :, n * G_LOW:n * G_LOW + GR]
            return piece(name, wt[name][:, n, :], k)

        def staged(name, k):
            if name == "gates":
                return stage[name].rearrange("p (k f) -> p k f", k=KC)
            return piece(name, stage[name], k)

        def bank(name):
            return work[bank_no(name)]

        def free_of(name):
            return work_free[bank_no(name)]

        def wait_bank(eng, i, name):
            n, b = USES.index(name), bank_no(name)
            eng.wait_ge(work_free[b], START + i * uses_of(b) + uses_of(b, n))

        def wait_full(eng, i, name):
            eng.wait_ge(work_full, i * NUSE + USES.index(name) + 1)

        def wait_drained(eng, i, name):
            b = bank_no(name)
            eng.wait_ge(work_free[b], START + i * uses_of(b) + uses_of(b, USES.index(name)) + 1)

        block = ctx.enter_context(nc.Block())
        x_blocks = x.rearrange("(i c p) d -> i p c d", c=NCH, p=P)
        out_blocks = out.rearrange("(i c p) d -> i p c d", c=NCH, p=P)

        @block.sync
        def _(sp):
            sp.dma_start(bias[:, :], gate_bias).then_inc(small_loaded, 16)
            sp.dma_start(gam[:, :], gamma).then_inc(small_loaded, 16)

            def load(n):
                step = WCOLS[n] // PIECES[n]
                for k in range(PIECES[n]):
                    span = slice(k * step, (k + 1) * step)
                    sp.dma_start(stage[n][:, span], w_dram[n][:, span]).then_inc(w_loaded[n][k], 16)

            for n in ROUNDS[0]:
                load(n)
            sp.dma_start(xin, x_blocks[0, :, :, :]).then_inc(x_loaded, 16)
            for n in ("g", "u"):
                load(n)
            sp.wait_ge(w_split, split_before("g"))
            sp.wait_ge(w_split_pool, pool_split_before("g"))
            load("out")
            load("d")
            with sp.Fori(0, NB) as i:
                sp.wait_ge(res_copied, NCH * (i + 1))
                sp.dma_start(xin, x_blocks[bass.ds((i + 1) % NB, 1), :, :, :]).then_inc(x_loaded, 16)
                sp.wait_ge(res_done, START + NCH * (i + 1))
                sp.dma_start(out_blocks[bass.ds(i, 1), :, :, :], res).then_inc(out_stored, 16)
            sp.wait_ge(x_loaded, 16 * (NB + 1))
            sp.wait_ge(out_stored, START + 16 * NB)

        @block.gpsimd
        def _(pool):
            g = nc.gpsimd
            own_k = [0]

            def link(ins):
                own_k[0] += 1
                ins.then_inc(pool_set, 1)
                pool.wait_ge(pool_set, own_k[0])

            def norm_factors(i, own):
                own.step(g.tensor_tensor(rstd, mean_var[:, :, 1], ln_eps[:, :], ALU.add))
                own.settle(pool, i)
                own.step(g.tensor_tensor(rstd, rstd, half_pow[:, 0:NCH], ALU.pow))
                own.settle(pool, i)
                own.step(g.tensor_tensor(shift, rstd, minus_xs[:, :], ALU.mult))
                own.settle(pool, i)
                own.step(g.tensor_tensor(rstd, rstd, xs[:, :], ALU.mult))
                g.tensor_tensor(shift, shift, mean_var[:, :, 0], ALU.mult).then_inc(factors_ready, 1)

            link(g.memset(m_carry, 0.0))
            link(g.memset(ident[:, :], 0.0))
            link(g.affine_select(out=ident[:, :], in_=ident[:, :], compare_op=ALU.not_equal, fill=1.0, base=0,
                                 pattern=[[-1, P]], channel_multiplier=1))
            link(g.memset(spread[:, :, :].bitcast(F32), 0.0))
            spread4 = spread[:, :, :].rearrange("p g (h d) -> p g h d", h=HG)
            for first in (0, 32):
                link(g.affine_select(out=spread4, in_=spread4.bitcast(F32), compare_op=ALU.not_equal, fill=1.0,
                                     base=-first, pattern=[[-HG, NG], [-1, HG], [0, DQ]], channel_multiplier=1))
            link(g.memset(we_r[:, :].bitcast(F32), 0.0))
            link(g.memset(w_gates[:, :, GR:G_LOW], 0.0))
            link(g.memset(diag[:, :], 0.0))
            for first in (0, 32):
                link(g.affine_select(out=diag[:, :], in_=diag[:, :], compare_op=ALU.not_equal, fill=1.0, base=-first,
                                     pattern=[[-1, NH]], channel_multiplier=1))
            link(g.memset(pair_r[:, :, :].bitcast(F32), 0.0))
            for first in (64, 96):
                link(g.affine_select(out=pair_r[:, :, :], in_=pair_r[:, :, :].bitcast(F32),
                                     compare_op=ALU.not_equal, fill=1.0, base=-first,
                                     pattern=[[-1, NH], [0, P]], channel_multiplier=1))
            link(g.memset(pair_l[:, :].bitcast(F32), 0.0))
            link(g.memset(pair_l[0:NH, :].bitcast(F32), -1.0))
            link(g.memset(pair_l[32:32 + NH, :].bitcast(F32), -1.0))
            link(g.memset(own_head[:, :], 0.0))
            for h in range(HG):
                link(g.memset(own_head[h * DQ:(h + 1) * DQ, h * VW:(h + 1) * VW], 1.0))
            link(g.memset(restart[:, :], 1.0))
            link(g.memset(restart[:, 0:BLOCK:P], 0.0))
            link(g.memset(keep[:, :], 1.0))
            link(g.memset(keep[:, 0:NB + 1:PER_SEQ], 0.0))
            link(g.memset(ln_eps[:, :], LN_EPS))
            link(g.memset(xs[:, :], XS))
            link(g.memset(minus_xs[:, :], -XS))
            g.memset(half_pow[:, :], -0.5).then_inc(consts, 1)

            def pool_low_parts(r):
                for name in ROUNDS[r]:
                    if name == "u":
                        pool.wait_ge(w_split, split_before(name))
                        pool.wait_ge(w_split_pool, pool_split_before(name))
                    for k in range(dve_pieces(name), PIECES[name]):
                        pool.wait_ge(w_hi, pieces_before(name, k) + 1)
                        g.tensor_tensor(part(name, 1, k), staged(name, k), part(name, 0, k),
                                        ALU.subtract).then_inc(w_split_pool, 1)

            for n, started in enumerate((*work_free, out_stored, res_done, exp_done, p_ready, num_ready, ho_ready,
                                         state_ready, xn_turned)):
                g.memset(begun[0:1, n:n + 1], 0.0).then_inc(started, START)
            for name in ("qq", "kk", "wr", "tg", "state"):
                link(g.memset(at[name], 0.0))
            link(g.memset(uhl.bitcast(F32), 0.0))
            for r, names in enumerate(ROUNDS):
                a, b = pieces_before(names[0]), pieces_before(names[-1], PIECES[names[-1]])
                pool.wait_ge(w_max, r + 1)
                g.partition_all_reduce(amax_pieces[:, a:b], amax[:, a:b], P, R_MAX).then_inc(w_max_all, 1)
                if r == 0:
                    pool.wait_ge(stats_ready, NCH)
                    first = Count(pool_set, 0)
                    first.k = own_k[0]
                    norm_factors(0, first)
                    own_k[0] = first.k
                if r == 0:
                    pool_low_parts(0)
                elif r == 2:
                    pool_low_parts(1)
            pool_low_parts(2)
            pool_low_parts(3)
            pool.wait_ge(w_split, split_before("d", dve_pieces("d")))
            link(g.memset(v[:, :, :, DV:DV + 1], 1.0))
            g.memset(v[:, :, :, DV + 1:VW], 0.0).then_inc(ready_set, 1)
            pool.wait_ge(ready_set, 1)

            with pool.Fori(0, NB) as i:
                own = Count(pool_own, 8)

                def pair(c):
                    g.tensor_tensor(pair_r[0:GR, :, :],
                                    uhl[0:GR, c * P:(c + 1) * P].bitcast(F32).unsqueeze(1).broadcast_to((GR, NH, P)),
                                    diag[0:GR, :].unsqueeze(2).broadcast_to((GR, NH, P)),
                                    ALU.mult).then_inc(pair_ready, 1)

                pool.wait_ge(parts_ready, i + 1)
                pair(0)
                for j in range(NJ):
                    pool.wait_ge(h_hi, i * NJ + j + 1)
                    g.tensor_tensor(hh[:, j % HB, 1, :], tt[:, j % 2, :], hh[:, j % HB, 0, :],
                                    ALU.subtract).then_inc(h_ready, 1)
                    for step in AFTER[j]:
                        if step.startswith("es"):
                            k = int(step[-1])
                            pool.wait_ge(exp_done, START + i * 4 + k + 1)
                            own.step(g.tensor_tensor(begun[0:1, 15:16], half_pow[0:1, 0:1], half_pow[0:1, 1:2],
                                                     ALU.add))
                            rows = pm[:, k % 2, :].rearrange("p (h t) -> p h t", h=HG)
                            g.affine_select(out=rows, in_=rows, compare_op=ALU.is_ge, fill=0.0, base=0,
                                            pattern=[[0, HG], [1, P]], channel_multiplier=-1).then_inc(masked, 1)
                        if step == "es1":
                            pool.wait_ge(e_full, i * 4 + 2)
                            pair(1)
                        if step.startswith("scale"):
                            pool.wait_ge(var_ready, i * NCH + int(step[-1]) + 1)
                            g.tensor_tensor(rd, var, half_pow[:, :], ALU.pow).then_inc(rd_ready, 1)
                        if step == "mean_var":
                            pool.wait_ge(stats_ready, NCH * (i + 2))
                            norm_factors(i, own)
                own.close()

        @block.scalar
        def _(act):
            s = nc.scalar

            def high_parts(r):
                act.wait_ge(w_scaled, r + 1)
                for name in ROUNDS[r]:
                    scale = wscale[:, sc[name]:sc[name] + 1]
                    if name in ("u", "d"):
                        before = {"u": "g", "d": "u"}[name]
                        half = PIECES[name] // 2
                        act.wait_ge(w_split, split_before(before, min(dve_pieces(before), half)))
                        if dve_pieces(before) < half:
                            act.wait_ge(w_split_pool, pool_split_before(before, half - dve_pieces(before)))
                    for k in range(PIECES[name]):
                        w = staged(name, k)
                        if k >= dve_pieces(name):
                            s.activation(w, w, ACT.Copy, scale=scale).then_inc(w_in_place, 1)
                            act.wait_ge(w_in_place, pool_split_before(name, k - dve_pieces(name)) + 1)
                            s.activation(part(name, 0, k), w, ACT.Copy).then_inc(w_hi, 1)
                        else:
                            s.activation(part(name, 0, k), w, ACT.Copy, scale=scale).then_inc(w_hi, 1)

            def x_high(i, c, src):
                s.activation(xt[:, :, 0, c * P:(c + 1) * P], src.rearrange("p (k t) -> p k t", k=KC),
                             ACT.Copy).then_inc(xt_hi, 1)

            def norm_x(i, c):
                act.wait_ge(factors_ready, i + 1)
                s.activation(xn, xin[:, c, :], ACT.Identity, bias=shift[:, c:c + 1],
                             scale=rstd[:, c:c + 1]).then_inc(xn_ready, 1)

            high_parts(0)
            for c in range(NCH):
                norm_x(0, c)
                act.wait_ge(first_xt, c + 1)
                x_high(0, c, (e_bank, s_bank)[c][:, :])
            for r in range(1, len(ROUNDS)):
                high_parts(r)
            act.wait_ge(w_unscaled, 1)
            act.wait_ge(ready_set, 1)

            with act.Fori(0, NB) as i:
                own = Count(act_own, 2)
                wait_full(act, i, "gates")
                s.activation(lf[0:GR, :], bank("gates")[G_LOW:G_LOW + GR, 0:BLOCK], ACT.Copy).then_inc(gates_low, 1)
                wait_drained(act, i, "gates")
                own.step(s.activation(tg[0:GR, :], lf[0:GR, :], ACT.Tanh, bias=bias[:, 0:1],
                                      scale=unscale[0:GR, 0:1]))
                own.settle(act, i)
                own.step(s.activation(lf[0:NH, :], tg[32:32 + NH, :], ACT.Exp, scale=-CAP))
                own.settle(act, i)
                s.activation(lf[0:NH, :], lf[0:NH, :], ACT.Ln, bias=1.0).then_inc(log_f_ready, 1)
                wait_full(act, i, "q")
                s.activation(at["qs"], bank("q")[:, :], ACT.Copy,
                             scale=unscale[:, NS:NS + 1]).then_inc(free_of("q"), 1)
                wait_full(act, i, "k")
                s.activation(at["kf"], bank("k")[:, :], ACT.Copy,
                             scale=unscale[:, sc["qk"]:sc["qk"] + 1]).then_inc(free_of("k"), 1)
                wait_drained(act, i, "k")
                s.activation(qp[:, 0, :, :], qs, ACT.Copy, scale=unscale[:, NS + 2:NS + 3]).then_inc(qk_hi, 1)
                s.activation(kp[:, 0, :, :], kf, ACT.Copy, scale=unscale[:, NS + 2:NS + 3]).then_inc(qk_hi, 1)
                for c in range(NCH):
                    wait_full(act, i, f"v{c}")
                    s.activation(v[:, c, :, 0:DV], bank(f"v{c}")[:, :].rearrange("p (h e) -> p h e", h=NH), ACT.Copy,
                                 scale=unscale[:, sc["v"]:sc["v"] + 1]).then_inc(free_of(f"v{c}"), 1)
                act.wait_ge(out_stored, START + 16 * i)
                act.wait_ge(x_loaded, 16 * (i + 1))
                for c in range(NCH):
                    s.activation(res[:, c, :], xin[:, c, :], ACT.Copy).then_inc(res_copied, 1)
                for j in range(NJ):
                    wait_full(act, i, f"ffn{j}")
                    if j >= 2:
                        act.wait_ge(h_ready, i * NJ + j - 1)
                    s.activation(tt[:, j % 2, :], bank(f"ffn{j}")[:, 0:BLOCK], ACT.Tanh,
                                 scale=unscale[:, sc["g"]:sc["g"] + 1]).then_inc(tanh_done, 1)
                    wait_drained(act, i, f"ffn{j}")
                    s.activation(hh[:, j % HB, 0, :], tt[:, j % 2, :], ACT.Copy).then_inc(h_hi, 1)
                    if j == 2:
                        act.wait_ge(rows_ready, i + 1)
                        s.activation(we[0:72, :], wr[0:72, :], ACT.Exp).then_inc(we_ready, 1)
                    for step in AFTER[j]:
                        k = int(step[-1]) if step[-1].isdigit() else 0
                        if step == "wT":
                            wait_full(act, i, "wT")
                            s.activation(at["wtok"], bank("wT")[:, 0:NCH * 72], ACT.Copy).then_inc(free_of("wT"), 1)
                        elif step.startswith("es"):
                            act.wait_ge(e_full, i * 4 + k + 1)
                            if k >= 2:
                                act.wait_ge(pv_full, i * 4 + k - 1)
                            s.activation(pm[:, k % 2, :], e_bank[:, :], ACT.Exp).then_inc(exp_done, 1)
                        elif step in ("o0", "o1"):
                            wait_full(act, i, step)
                            act.wait_ge(ho_ready, START + i * NCH + k)
                            s.activation(to, bank(step)[:, :], ACT.Tanh,
                                         scale=unscale[:, sc["o"]:sc["o"] + 1]).then_inc(free_of(step), 1)
                        elif step.startswith("pv"):
                            act.wait_ge(pv_full, i * 4 + k + 1)
                            act.wait_ge(ho_ready, START + i * NCH + k // 2)
                            s.activation(num[:, HG * (k % 2):HG * (k % 2) + HG, :],
                                         o_bank[:, 0:GW].rearrange("p (h e) -> p h e", h=HG),
                                         ACT.Copy).then_inc(num_ready, 1)
                        elif step.startswith("center"):
                            act.wait_ge(centered, i * NCH + k + 1)
                            s.activation(sq, num[:, :, 0:DV], ACT.Square).then_inc(squared, 1)
                        elif step == "hoT0":
                            act.wait_ge(ho_turned, (i + 1) * TURNS)
                            s.activation(ho[:, 0, :, :], xnt[:, 1, :, :], ACT.Copy).then_inc(ho_hi, 1)
                        elif step == "hoT1":
                            wait_full(act, i, step)
                            s.activation(ho[:, 0, :, :], bank(step)[:, :].rearrange("p (k t) -> p k t", k=KC),
                                         ACT.Copy).then_inc(ho_hi, 1)
                        elif step.startswith("xn"):
                            act.wait_ge(xn_turned, START + i * NCH * TURNS + k * TURNS)
                            norm_x(i + 1, k)
                        elif step.startswith("xT"):
                            act.wait_ge(xn_turned, START + i * NCH * TURNS + (k + 1) * TURNS)
                            s.activation(xt[:, :, 0, k * P:(k + 1) * P], xnt[:, k, :, :], ACT.Copy).then_inc(xt_hi, 1)
                own.close()

        @block.vector
        def _(dve):
            d = nc.vector
            k = [0]

            def link(ins):
                k[0] += 1
                ins.then_inc(dve_set, 1)
                dve.wait_ge(dve_set, k[0])

            def maxima(r):
                if ROUNDS[r] == ["out"]:
                    dve.wait_ge(w_loaded["out"][0], 16)
                    for c in range(KC):
                        w = stage["out"][:, c * D:(c + 1) * D]
                        d.tensor_scalar(w, w, gam[:, c:c + 1], None, ALU.mult).then_inc(w_gamma, 1)
                    dve.wait_ge(w_gamma, KC)
                for name in ROUNDS[r]:
                    for k in range(PIECES[name]):
                        dve.wait_ge(w_loaded[name][k], 16)
                        ins = d.tensor_reduce(amax_of(name, k), piece(name, stage[name], k), AX.X, ALU.max,
                                              apply_absolute_value=True)
                        if name == ROUNDS[r][-1] and k == PIECES[name] - 1:
                            ins.then_inc(w_max, 1)
                        else:
                            link(ins)

            def scales(r):
                a, b = sc[ROUNDS[r][0]], sc[ROUNDS[r][-1]] + 1
                dve.wait_ge(w_max_all, r + 1)
                n = pieces_before(ROUNDS[r][0])
                if PIECES[ROUNDS[r][0]] > 1:
                    link(d.tensor_reduce(amax_all[:, a:b], amax_pieces[:, n:n + PIECES[ROUNDS[r][0]]], AX.X,
                                         ALU.max))
                    link(d.tensor_scalar(amax_all[:, a:b], amax_all[:, a:b], 1e-30, None, ALU.max))
                else:
                    link(d.tensor_scalar(amax_all[:, a:b], amax_pieces[:, n:n + b - a], 1e-30, None, ALU.max))
                link(d.tensor_scalar(pow2[:, a:b].bitcast(I32), amax_all[:, a:b].bitcast(I32), 0x7F800000, None,
                                     ALU.bitwise_and))
                link(d.reciprocal(wscale[:, a:b], pow2[:, a:b]))
                d.tensor_scalar(wscale[:, a:b], wscale[:, a:b], WS, None, ALU.mult).then_inc(w_scaled, 1)
                dve.wait_ge(w_scaled, r + 1)

            def low_parts(r):
                for name in ROUNDS[r]:
                    if name in ("u", "d"):
                        dve.wait_ge(w_split, split_before(name))
                        dve.wait_ge(w_split_pool, pool_split_before("u" if name == "u" else "out"))
                    for k in range(dve_pieces(name)):
                        dve.wait_ge(w_hi, pieces_before(name, k) + 1)
                        d.scalar_tensor_tensor(out=part(name, 1, k), in0=staged(name, k),
                                               scalar=wscale[:, sc[name]:sc[name] + 1], in1=part(name, 0, k),
                                               op0=ALU.mult, op1=ALU.subtract).then_inc(w_split, 1)

            def stats(step):
                for c in range(NCH):
                    step(d.bn_stats(bn6[:, c, :], xin[:, c, :]))

            def means():
                for c in range(NCH):
                    d.bn_aggr(mean_var[:, c, :], bn6[:, c, :]).then_inc(stats_ready, 1)

            def x_low(i, c, src):
                dve.wait_ge(xt_hi, NCH * i + c + 1)
                d.tensor_tensor(xt[:, :, 1, c * P:(c + 1) * P], src, xt[:, :, 0, c * P:(c + 1) * P],
                                ALU.subtract).then_inc(xt_ready, 1)

            maxima(0)
            scales(0)
            dve.wait_ge(x_loaded, 16)
            stats(link)
            means()

            back = 1.0 / (XS * WS)

            def factor(name, f):
                link(d.tensor_scalar(unscale[:, sc[name]:sc[name] + 1], pow2[:, sc[name]:sc[name] + 1], f, None,
                                     ALU.mult))

            for name, f in (("gates", back / CAP), ("qk", back), ("v", back), ("o", back / 2)):
                factor(name, f)
            link(d.tensor_scalar(unscale[:, NS:NS + 1], unscale[:, sc["qk"]:sc["qk"] + 1], float(DQ) ** -0.5, None,
                                 ALU.mult))
            link(d.tensor_scalar(unscale[:, NS + 2:NS + 3], wscale[:, sc["qk"]:sc["qk"] + 1], QKS / WS, None,
                                 ALU.mult))
            link(d.tensor_scalar(unscale[:, NS + 3:NS + 4], pow2[:, sc["qk"]:sc["qk"] + 1], 1.0 / QKS, None,
                                 ALU.mult))
            link(d.tensor_tensor(unscale[:, NS + 3:NS + 4], unscale[:, NS + 3:NS + 4], unscale[:, NS + 3:NS + 4],
                                 ALU.mult))
            dve.wait_ge(small_loaded, 32)
            link(d.tensor_scalar(bias[:, :], bias[:, :], 1.0 / CAP, None, ALU.mult))
            low_parts(0)
            maxima(1)
            scales(1)
            maxima(2)
            for c in range(NCH):
                x_low(0, c, (e_bank, s_bank)[c][:, :].rearrange("p (k t) -> p k t", k=KC))
            low_parts(1)
            scales(2)
            maxima(3)
            maxima(4)
            scales(3)
            scales(4)
            low_parts(2)

            factor("g", back / 2)
            factor("out", 1.0 / (WS * OS * 2))
            link(d.tensor_tensor(unscale[:, NS + 1:NS + 2], pow2[:, sc["g"]:sc["g"] + 1],
                                 pow2[:, sc["u"]:sc["u"] + 1], ALU.mult))
            link(d.tensor_tensor(unscale[:, NS + 1:NS + 2], unscale[:, NS + 1:NS + 2],
                                 pow2[:, sc["d"]:sc["d"] + 1], ALU.mult))
            d.tensor_scalar(unscale[:, NS + 1:NS + 2], unscale[:, NS + 1:NS + 2], 2.0 ** 5 / WS, None,
                            ALU.mult).then_inc(w_unscaled, 1)

            low_parts(3)
            low_parts(4)

            def add_mlstm(i, c):
                wait_full(dve, i, f"att{c}")
                dve.wait_ge(res_copied, i * NCH + c + 1)
                d.scalar_tensor_tensor(out=res[:, c, :], in0=bank(f"att{c}")[:, :],
                                       scalar=unscale[:, sc["out"]:sc["out"] + 1], in1=res[:, c, :],
                                       op0=ALU.mult, op1=ALU.add).then_inc(free_of(f"att{c}"), 1)

            with dve.Fori(0, NB) as i:
                own = Count(dve_own, DVE_OWN)

                def turn(dst, src, q, turned):
                    tokens = slice(q * 32, (q + 1) * 32)
                    for r in range(P // 32):
                        features = src[tokens, :].rearrange("t (k r f) -> t r k f", k=KC, f=32)[:, r, :, :]
                        d.transpose(dst[r * 32:(r + 1) * 32, :, tokens], features).then_inc(turned, 1)

                def stack(h):
                    rows = slice(h * DQ, (h + 1) * DQ)
                    for n, (q_part, k_part) in enumerate(((0, 0), (1, 0), (0, 1))):
                        to_ = slice((h + n) % HG * DQ, ((h + n) % HG + 1) * DQ)
                        d.tensor_copy(qq[to_, :, h, :], qp[rows, q_part, :, :]).then_inc(stacks_ready, 1)
                        d.tensor_copy(kk[to_, :, h, :], kp[rows, k_part, :, :]).then_inc(stacks_ready, 1)

                dve.wait_ge(gates_low, i + 1)
                d.tensor_tensor(lf[0:GR, :], bank("gates")[0:GR, 0:BLOCK], lf[0:GR, :],
                                ALU.add).then_inc(free_of("gates"), 1)
                dve.wait_ge(log_f_ready, i + 1)
                own.step(d.tensor_scalar(lf[0:NH, :], lf[0:NH, :], -1.0, None, ALU.mult))
                own.step(d.tensor_scalar(ip[0:NH, :], tg[0:NH, :], CAP, None, ALU.mult))
                own.settle(dve, i)
                own.step(d.tensor_tensor_scan(bc[0:NH, :], restart[:, :], lf[0:NH, :], 0.0, ALU.mult, ALU.add))
                own.step(d.tensor_tensor_scan(mm[0:NH, :], lf[0:NH, :], ip[0:NH, :], m_carry, ALU.add, ALU.max))
                own.settle(dve, i)
                own.step(d.tensor_tensor(aa[0:NH, :], ip[0:NH, :], bc[0:NH, :], ALU.subtract))
                own.settle(dve, i)
                own.step(d.tensor_tensor(uu[0:NH, :], mm[0:NH, :], bc[0:NH, :], ALU.subtract))
                own.settle(dve, i)
                for c in range(NCH):
                    span, end = slice(c * P, (c + 1) * P), c * P + P - 1
                    prev = m_carry if c == 0 else mm[0:NH, c * P - 1:c * P]
                    own.step(d.tensor_scalar(wr[0:NH, span], uu[0:NH, span], prev, -1.0, ALU.subtract, ALU.mult))
                    own.step(d.tensor_scalar(wr[32:32 + NH, span], aa[0:NH, span], uu[0:NH, end:end + 1], None,
                                             ALU.subtract))
                d.tensor_scalar(wr[64:64 + NH, :], mm[0:NH, :], -1.0, None, ALU.mult).then_inc(rows_ready, 1)
                own.step(d.tensor_copy(uhl[0:NH, :], uu[0:NH, :]))
                own.step(d.tensor_copy(a_hi[0:NH, :], aa[0:NH, :]))
                own.step(d.tensor_copy(pair_l[64:64 + NH, :], aa[0:NH, :]))
                own.settle(dve, i)
                own.step(d.tensor_scalar(m_carry, mm[0:NH, BLOCK - 1:BLOCK], keep[0:NH, bass.ds(i + 1, 1)], None,
                                         ALU.mult))
                own.step(d.tensor_tensor(uhl[32:32 + NH, :], uu[0:NH, :], uhl[0:NH, :].bitcast(F32), ALU.subtract))
                d.tensor_tensor(pair_l[96:96 + NH, :], aa[0:NH, :], a_hi[0:NH, :].bitcast(F32),
                                ALU.subtract).then_inc(parts_ready, 1)
                dve.wait_ge(qk_hi, 2 * (i + 1))
                own.step(d.scalar_tensor_tensor(out=qp[:, 1, :, :], in0=qs, scalar=unscale[:, NS + 2:NS + 3],
                                                in1=qp[:, 0, :, :], op0=ALU.mult, op1=ALU.subtract))
                own.step(d.scalar_tensor_tensor(out=kp[:, 1, :, :], in0=kf, scalar=unscale[:, NS + 2:NS + 3],
                                                in1=kp[:, 0, :, :], op0=ALU.mult, op1=ALU.subtract))
                own.settle(dve, i)
                stack(0)
                stack(1)
                stack(2)

                for j in range(NJ):
                    b = bank(f"ffn{j}")
                    dve.wait_ge(tanh_done, i * NJ + j + 1)
                    own.step(d.scalar_tensor_tensor(out=tt[:, j % 2, :], in0=tt[:, j % 2, :], scalar=1.0,
                                                    in1=b[:, 0:BLOCK], op0=ALU.add, op1=ALU.mult))
                    own.settle(dve, i)
                    d.scalar_tensor_tensor(out=tt[:, j % 2, :], in0=tt[:, j % 2, :], scalar=HS,
                                           in1=b[:, BLOCK:2 * BLOCK], op0=ALU.mult,
                                           op1=ALU.mult).then_inc(free_of(f"ffn{j}"), 1)
                    for step in AFTER[j]:
                        k_ = int(step[-1]) if step[-1].isdigit() else 0
                        if step == "stack3":
                            stack(3)
                        elif step == "stats":
                            dve.wait_ge(x_loaded, 16 * (i + 2))
                            stats(own.step)
                        elif step == "wT":
                            dve.wait_ge(we_ready, i + 1)
                            own.step(d.tensor_copy(we_r[0:NH, :], we[0:NH, :]))
                            own.settle(dve, i)
                            d.tensor_tensor(we_r[32:32 + NH, :], we[0:NH, :], we_r[0:NH, :].bitcast(F32),
                                            ALU.subtract).then_inc(we_split, 1)
                        elif step == "mean_var":
                            means()
                        elif step == "wbc":
                            wb = bank("wbc")[:, :].rearrange("p (g t) -> p g t", g=NG)
                            wait_full(dve, i, "wbc")
                            wait_drained(dve, i, "q")
                            d.tensor_tensor(at["qi"], at["qs"], bank("wbc")[:, :], ALU.mult).then_inc(qi_ready, 1)
                            d.tensor_copy(decay, wb[:, :, P - 1:BLOCK:P]).then_inc(free_of("wbc"), 1)
                        elif step == "kT":
                            wait_full(dve, i, "kT")
                            wait_drained(dve, i, "wT")
                            d.tensor_tensor(kt[:, :, :].rearrange("p c (h e) -> p c h e", h=NH),
                                            bank("kT")[:, :].rearrange("p (c h e) -> p c h e", c=NCH, h=NH),
                                            wtok[:, :, 32:32 + NH].unsqueeze(3).broadcast_to((P, NCH, NH, DQ)),
                                            ALU.mult).then_inc(free_of("kT"), 1)
                        elif step.startswith("es"):
                            dve.wait_ge(s_full, i * 4 + k_ + 1)
                            dve.wait_ge(masked, i * 4 + k_ + 1)
                            d.scalar_tensor_tensor(out=pm[:, k_ % 2, :], in0=s_bank[:, :],
                                                   scalar=unscale[:, NS + 3:NS + 4], in1=pm[:, k_ % 2, :],
                                                   op0=ALU.mult, op1=ALU.mult).then_inc(p_ready, 1)
                        elif step.startswith("pv"):
                            c, g = k_ // 2, k_ % 2
                            wait_full(dve, i, f"st{k_}")
                            wait_drained(dve, i, "wbc")
                            d.tensor_tensor(upd, own_head[:, :], bank(f"st{k_}")[:, 0:GW],
                                            ALU.mult).then_inc(free_of(f"st{k_}"), 1)
                            wait_drained(dve, i, f"st{k_}")
                            d.scalar_tensor_tensor(out=state[:, g, :], in0=state[:, g, :],
                                                   scalar=decay[:, g, c:c + 1], in1=upd, op0=ALU.mult,
                                                   op1=ALU.add).then_inc(state_ready, 1)
                            if k_ == 3:
                                dve.wait_ge(state_ready, START + i * 5 + 4)
                                d.tensor_scalar(at["state"], at["state"], keep[:, bass.ds(i + 1, 1)], None,
                                                ALU.mult).then_inc(state_ready, 1)
                        elif step.startswith("center"):
                            dve.wait_ge(num_ready, START + i * 4 + 2 * k_ + 2)
                            own.step(d.tensor_reduce(hsum, num[:, :, 0:DV], AX.X, ALU.add))
                            own.settle(dve, i)
                            own.step(d.tensor_scalar(mu, hsum, 1.0 / DV, None, ALU.mult))
                            own.settle(dve, i)
                            d.tensor_tensor(num[:, :, 0:DV], num[:, :, 0:DV],
                                            mu.unsqueeze(2).broadcast_to((P, NH, DV)),
                                            ALU.subtract).then_inc(centered, 1)
                            own.step(d.scalar_tensor_tensor(out=den, in0=num[:, :, DV], scalar=-1.0,
                                                            in1=wtok[:, k_, 64:64 + NH], op0=ALU.mult, op1=ALU.max))
                            own.settle(dve, i)
                            own.step(d.tensor_tensor(den, den, num[:, :, DV], ALU.max))
                            own.settle(dve, i)
                            own.step(d.tensor_scalar(den, den, EPS, None, ALU.add))
                            own.settle(dve, i)
                            own.step(d.reciprocal(rden, den))
                        elif step.startswith("scale"):
                            dve.wait_ge(squared, i * NCH + k_ + 1)
                            own.step(d.tensor_reduce(vsum, sq, AX.X, ALU.add))
                            own.settle(dve, i)
                            own.step(d.tensor_tensor(vsum, vsum, rden, ALU.mult))
                            own.settle(dve, i)
                            own.step(d.tensor_tensor(vsum, vsum, rden, ALU.mult))
                            own.settle(dve, i)
                            d.tensor_scalar(var, vsum, 1.0 / DV, EPS, ALU.mult, ALU.add).then_inc(var_ready, 1)
                        elif step.startswith("heads"):
                            dve.wait_ge(rd_ready, i * NCH + k_ + 1)
                            own.step(d.scalar_tensor_tensor(out=fac, in0=rden, scalar=OS, in1=rd, op0=ALU.mult,
                                                            op1=ALU.mult))
                            own.settle(dve, i)
                            own.step(d.tensor_tensor(num[:, :, 0:DV], num[:, :, 0:DV],
                                                     fac.unsqueeze(2).broadcast_to((P, NH, DV)), ALU.mult))
                            own.settle(dve, i)
                            wait_drained(dve, i, f"o{k_}")
                            d.scalar_tensor_tensor(out=hof.rearrange("p (h e) -> p h e", h=NH),
                                                   in0=to.rearrange("p (h e) -> p h e", h=NH), scalar=1.0,
                                                   in1=num[:, :, 0:DV], op0=ALU.add,
                                                   op1=ALU.mult).then_inc(ho_ready, 1)
                        elif step.startswith("hoTurn"):
                            if k_ == 0:
                                dve.wait_ge(ho_ready, START + i * NCH + 1)
                            turn(xnt[:, 1, :, :], hof, k_, ho_turned)
                        elif step == "hoT0":
                            dve.wait_ge(ho_hi, i * NCH + 1)
                            d.tensor_tensor(ho[:, 1, :, :], xnt[:, 1, :, :], ho[:, 0, :, :],
                                            ALU.subtract).then_inc(ho_split, 1)
                        elif step == "hoT1":
                            dve.wait_ge(ho_hi, i * NCH + k_ + 1)
                            d.tensor_tensor(ho[:, 1, :, :], bank(step)[:, :].rearrange("p (k t) -> p k t", k=KC),
                                            ho[:, 0, :, :], ALU.subtract).then_inc(free_of(step), 1)
                        elif step.startswith("turn"):
                            c = int(step[-2])
                            dve.wait_ge(xn_ready, NCH * (i + 1) + c + 1)
                            if (c, k_) == (1, 0):
                                dve.wait_ge(ho_split, i + 1)
                            turn(xnt[:, c, :, :], xn, k_, xn_turned)
                        elif step.startswith("xT"):
                            x_low(i + 1, k_, xnt[:, k_, :, :])
                        elif step == "att0":
                            add_mlstm(i, 0)
                for c in range(NCH):
                    if c == 1:
                        add_mlstm(i, 1)
                    dve.wait_ge(acc_full, i * NCH + c + 1)
                    wait_drained(dve, i, f"att{c}")
                    d.scalar_tensor_tensor(out=res[:, c, :], in0=acc[c][:, :], scalar=unscale[:, NS + 1:NS + 2],
                                           in1=res[:, c, :], op0=ALU.mult, op1=ALU.add).then_inc(res_done, 1)
                own.close()

        @block.tensor
        def _(pe):
            t = nc.tensor

            def three(dst, w, a, first, last):
                t.matmul(dst, w[0], a[0], start=first, stop=False, skip_group_check=True)
                t.matmul(dst, w[0], a[1], start=False, stop=False, skip_group_check=True)
                return t.matmul(dst, w[1], a[0], start=False, stop=last, skip_group_check=True)

            def by_feature(dst, w, f0, f1):
                for k in range(KC):
                    mm_ = three(dst, (w[:, 0, k, f0:f1], w[:, 1, k, f0:f1]), (xt[:, k, 0, :], xt[:, k, 1, :]),
                                k == 0, k == KC - 1)
                return mm_

            def by_token(dst, c, w):
                span = slice(c * P, (c + 1) * P)
                for k in range(KC):
                    mm_ = three(dst, (xt[:, k, 0, span], xt[:, k, 1, span]), (w[:, 0, k, :], w[:, 1, k, :]),
                                k == 0, k == KC - 1)
                return mm_

            pe.wait_ge(consts, 1)
            for c in range(NCH):
                pe.wait_ge(xn_ready, c + 1)
                for k in range(KC):
                    tr = t.transpose((e_bank, s_bank)[c][:, k * P:(k + 1) * P], xn[:, k * P:(k + 1) * P],
                                     ident[:, :])
                tr.then_inc(first_xt, 1)

            with pe.Fori(0, NB) as i:
                def down(j):
                    pe.wait_ge(h_ready, i * NJ + j + 1)
                    for c in range(NCH):
                        if j == 0:
                            pe.wait_ge(res_done, START + i * NCH)
                        span = slice(c * P, (c + 1) * P)
                        h = hh[:, j % HB, :, :]
                        mm_ = three(acc[c][:, :], (h[:, 0, span], h[:, 1, span]), (w_d[:, 0, j, :], w_d[:, 1, j, :]),
                                    j == 0, j == NJ - 1)
                        if j == NJ - 1:
                            mm_.then_inc(acc_full, 1)

                def project(c):
                    if c == 0:
                        pe.wait_ge(ho_split, i + 1)
                    else:
                        wait_drained(pe, i, "hoT1")
                    for n in range(KC):
                        mm_ = three(bank(f"att{c}")[:, :], (ho[:, 0, n, :], ho[:, 1, n, :]),
                                    (w_out[:, 0, n, :], w_out[:, 1, n, :]), n == 0, n == KC - 1)
                    mm_.then_inc(work_full, 1)

                pe.wait_ge(xt_ready, NCH * (i + 1))
                wait_bank(pe, i, "gates")
                for k in range(KC):
                    t.matmul(bank("gates")[0:G_LOW + GR, 0:BLOCK], w_gates[:, k, :], xt[:, k, 0, :], start=(k == 0),
                             stop=(k == KC - 1), skip_group_check=True)
                    mm_ = t.matmul(bank("gates")[0:GR, 0:BLOCK], w_gates[:, k, 0:GR], xt[:, k, 1, :], start=False,
                                   stop=(k == KC - 1), skip_group_check=True)
                mm_.then_inc(work_full, 1)
                for name, f in (("q", 0), ("k", NH * DQ)):
                    wait_bank(pe, i, name)
                    for g in range(NG):
                        mm_ = by_feature(bank(name)[:, g * BLOCK:(g + 1) * BLOCK], w_qk, f + g * P, f + (g + 1) * P)
                    mm_.then_inc(work_full, 1)
                for c in range(NCH):
                    wait_bank(pe, i, f"v{c}")
                    by_token(bank(f"v{c}")[:, :], c, w_v).then_inc(work_full, 1)

                for j in range(NJ):
                    name = f"ffn{j}"
                    wait_bank(pe, i, name)
                    if j in UNIT_IN:
                        pe.wait_ge(p_ready, START + i * 4 + UNIT_IN[j] + 1)
                    for k in range(KC):
                        if j in UNIT_IN:
                            c, g = UNIT_IN[j] // 2, UNIT_IN[j] % 2
                            mm_ = t.matmul(o_bank[:, k * VW:(k + 1) * VW], pm[:, UNIT_IN[j] % 2, k * P:(k + 1) * P],
                                           v[:, c, g * HG + k, :], start=False, stop=(k == HG - 1),
                                           skip_group_check=True)
                            if k == HG - 1:
                                mm_.then_inc(pv_full, 1)
                        w = (w_g[:, 0, k, j * P:(j + 1) * P], w_g[:, 1, k, j * P:(j + 1) * P])
                        three(bank(name)[:, 0:BLOCK], w, (xt[:, k, 0, :], xt[:, k, 1, :]), k == 0, k == KC - 1)
                    by_feature(bank(name)[:, BLOCK:2 * BLOCK], w_u, j * P, (j + 1) * P).then_inc(work_full, 1)
                    if j >= 2:
                        down(j - 2)
                    for step in AFTER[j]:
                        k = int(step[-1]) if step[-1].isdigit() else 0
                        if step in USES:
                            wait_bank(pe, i, step)
                        if step == "wT":
                            pe.wait_ge(we_ready, i + 1)
                            for c in range(NCH):
                                tr = t.transpose(bank(step)[:, c * 72:(c + 1) * 72], we[0:72, c * P:(c + 1) * P],
                                                 ident[0:72, 0:72])
                            tr.then_inc(work_full, 1)
                        elif step == "wbc":
                            pe.wait_ge(we_split, i + 1)
                            for g in range(NG):
                                mm_ = t.matmul(bank(step)[:, g * BLOCK:(g + 1) * BLOCK], spread[0:GR, g, :],
                                               we_r[:, :], start=True, stop=True)
                            mm_.then_inc(work_full, 1)
                        elif step == "kT":
                            wait_drained(pe, i, "k")
                            for c in range(NCH):
                                for g in range(NG):
                                    n = c * NG + g
                                    tr = t.transpose(bank(step)[:, n * P:(n + 1) * P], kf[:, g, c * P:(c + 1) * P],
                                                     ident[:, :])
                            tr.then_inc(work_full, 1)
                        elif step.startswith("es"):
                            c, g = k // 2, k % 2
                            span = slice(c * P, (c + 1) * P)
                            pe.wait_ge(pair_ready, i * NCH + c + 1)
                            pe.wait_ge(exp_done, START + i * 4 + k)
                            t.matmul(e_bank[:, :], pair_l[:, span], pair_r[:, g * HG:(g + 1) * HG, :], start=True,
                                     stop=True).then_inc(e_full, 1)
                            pe.wait_ge(stacks_ready, (i + 1) * 6 * HG)
                            pe.wait_ge(p_ready, START + i * 4 + k)
                            for h in range(HG):
                                mm_ = t.matmul(s_bank[:, h * P:(h + 1) * P], kk[:, g, h, span], qq[:, g, h, span],
                                               start=True, stop=True)
                            mm_.then_inc(s_full, 1)
                        elif step in ("o0", "o1"):
                            by_token(bank(step)[:, :], k, w_o).then_inc(work_full, 1)
                        elif step.startswith("pv"):
                            c, g = k // 2, k % 2
                            span = slice(c * P, (c + 1) * P)
                            pe.wait_ge(qi_ready, i + 1)
                            pe.wait_ge(state_ready, START + i * 5 + (k - 1 if c else 0))
                            pe.wait_ge(num_ready, START + i * 4 + k)
                            t.matmul(o_bank[:, 0:GW], qi[:, g, span], state[:, g, :], start=True, stop=False,
                                     skip_group_check=True)
                            wait_drained(pe, i, f"v{c}")
                            wait_bank(pe, i, f"st{k}")
                            wait_drained(pe, i, "kT")
                            t.matmul(bank(f"st{k}")[:, 0:GW], kt[:, c, g * P:(g + 1) * P],
                                     v[:, c, g * HG:(g + 1) * HG, :], start=True,
                                     stop=True).then_inc(work_full, 1)
                        elif step == "hoT1":
                            pe.wait_ge(ho_ready, START + i * NCH + k + 1)
                            for n in range(KC):
                                tr = t.transpose(bank(step)[:, n * P:(n + 1) * P], hof[:, n * P:(n + 1) * P],
                                                 ident[:, :])
                            tr.then_inc(work_full, 1)
                        elif step == "att0":
                            project(0)
                down(NJ - 2)
                down(NJ - 1)
                wait_bank(pe, i, "att1")
                project(1)


def kernel(L0_attn_x, L0_attn_Wq, L0_attn_Wk, L0_attn_Wv, L0_attn_Wog, L0_attn_Wig, L0_attn_big, L0_attn_Wfg,
           L0_attn_bfg, L0_attn_gamma, L0_attn_Wout, L0_ffn_w_gate, L0_ffn_w_up, L0_ffn_w_down):
    import numpy as np
    import concourse.bacc as bacc
    from concourse.bass_utils import run_bass_kernel_spmd

    def tiles(w):
        a = np.asarray(w).T
        return np.ascontiguousarray(a.reshape(-1, P, a.shape[1]).transpose(1, 0, 2)).reshape(P, -1)

    f32 = np.float32
    w_if = np.zeros((GR, D), f32)
    w_if[0:NH], w_if[32:32 + NH] = L0_attn_Wig, L0_attn_Wfg
    b_if = np.zeros((GR, 1), f32)
    b_if[0:NH, 0], b_if[32:32 + NH, 0] = L0_attn_big, L0_attn_bfg
    w_qk = np.concatenate([np.asarray(L0_attn_Wq), np.asarray(L0_attn_Wk)])
    arrays = {
        "x": np.ascontiguousarray(L0_attn_x).reshape(BATCH * SEQ, D),
        "w_gates": tiles(w_if), "w_qk": tiles(w_qk), "w_v": tiles(L0_attn_Wv), "w_o": tiles(L0_attn_Wog),
        "w_g": tiles(L0_ffn_w_gate), "w_u": tiles(L0_ffn_w_up), "w_d": tiles(L0_ffn_w_down),
        "w_out": tiles(L0_attn_Wout), "gate_bias": b_if,
        "gamma": np.ascontiguousarray(np.asarray(L0_attn_gamma).reshape(KC, P).T),
    }
    nc = bacc.Bacc("TRN2", target_bir_lowering=False, num_devices=1)
    ap = {n: nc.dram_tensor(f"{n}_dram", a.shape, F32, kind="ExternalInput").ap() for n, a in arrays.items()}
    out = nc.dram_tensor("out_dram", (BATCH * SEQ, D), F32, kind="ExternalOutput").ap()
    mlstm_mlp_kernel(nc, ap["x"], {n: ap[f"w_{n}"] for n in WNAMES}, ap["gate_bias"], ap["gamma"], out)
    got = run_bass_kernel_spmd(nc, [{f"{n}_dram": a for n, a in arrays.items()}], core_ids=[0])
    return got.results[0]["out_dram"].reshape(BATCH, SEQ, D)
```
